# Optimizing a Trainium2 kernel written in Bass

```python
import numpy as np
import jax
import jax.numpy as jnp

def _softmax(x, axis=-1):
    return jax.nn.softmax(x, axis=axis)
def _gelu(x):
    return jax.nn.gelu(x, approximate=True)
def _silu(x):
    return jax.nn.silu(x)
def _sigmoid(x):
    return jax.nn.sigmoid(x)
def _layernorm(x, axis=-1, eps=1e-5):
    m = jnp.mean(x, axis=axis, keepdims=True)
    v = jnp.var(x, axis=axis, keepdims=True)
    return (x - m) / jnp.sqrt(v + eps)
def _scatter_add(tgt, idx, src, axis=0):
    return tgt.at[idx].add(src)
def _segment_sum(src, seg, n):
    return jax.ops.segment_sum(src, seg, n)

kernel_name = 'mk_conv_preact_d4_conv_nchw96_755bfd'

def setup_inputs(seed: int = 0):
    np.random.seed(seed)
    _w = jnp.asarray
    def _rec_inputs():
        import jax
        import jax.numpy as jnp
        _gk = jax.random.key(seed)
        x = -0.0008768 + 1.001 * jax.random.normal(jax.random.fold_in(_gk, 1), (2, 96, 96, 96), jnp.float32)
        return x
    x = _rec_inputs()
    def _L0_conv_setup():
        import jax, jax.numpy as jnp
        import numpy as np
        import math
        D_MODEL = 96
        SSM_RATIO = 2.0
        D_INNER = int(SSM_RATIO * D_MODEL)
        N_STATE = 16
        R_DT = math.ceil(D_MODEL / 16)
        KG = 4
        B, H, W = (2, 96, 96)
        KERNEL = 16

        def _conv(x, w, pad):
            return jax.lax.conv_general_dilated(x, w, (1, 1), [(pad, pad), (pad, pad)], dimension_numbers=('NCHW', 'OIHW', 'NCHW'))

        def grid_sample_bilinear(img, grid):
            Bb, C, Hh, Ww = img.shape
            gx = (grid[..., 0] + 1.0) * 0.5 * (Ww - 1)
            gy = (grid[..., 1] + 1.0) * 0.5 * (Hh - 1)
            x0 = jnp.floor(gx)
            y0 = jnp.floor(gy)
            x1 = x0 + 1.0
            y1 = y0 + 1.0
            bidx = jnp.arange(Bb)[:, None, None]

            def gather(yi, xi):
                valid = (yi >= 0) & (yi <= Hh - 1) & (xi >= 0) & (xi <= Ww - 1)
                yc = jnp.clip(yi, 0, Hh - 1).astype(jnp.int32)
                xc = jnp.clip(xi, 0, Ww - 1).astype(jnp.int32)
                v = img[bidx, :, yc, xc]
                return v * valid[..., None]
            wa = ((x1 - gx) * (y1 - gy))[..., None]
            wb = ((gx - x0) * (y1 - gy))[..., None]
            wc = ((x1 - gx) * (gy - y0))[..., None]
            wd = ((gx - x0) * (gy - y0))[..., None]
            out = gather(y0, x0) * wa + gather(y0, x1) * wb + gather(y1, x0) * wc + gather(y1, x1) * wd
            return jnp.moveaxis(out, -1, 1)

        def selective_scan(u, delta, A, Bm, Cm, Dv):
            Bt, K_, Dd, L = u.shape
            N = A.shape[-1]
            us = jnp.moveaxis(u, -1, 0)
            ds = jnp.moveaxis(delta, -1, 0)
            bs = jnp.moveaxis(Bm, -1, 0)
            cs = jnp.moveaxis(Cm, -1, 0)

            def step(hst, inputs):
                ut, dt, bt, ct = inputs
                dA = jnp.exp(dt[..., None] * A)
                hst = hst * dA + (dt * ut)[..., None] * bt[:, :, None, :]
                y = jnp.einsum('bkdn,bkn->bkd', hst, ct)
                return (hst, y)
            h0 = jnp.zeros((Bt, K_, Dd, N), u.dtype)
            _, ys = jax.lax.scan(step, h0, (us, ds, bs, cs))
            return jnp.moveaxis(ys, 0, -1) + Dv[None, :, :, None] * u
        key = jax.random.key(seed)
        ks = jax.random.split(key, 10)
        f = jnp.float32
        dt = jnp.exp(jax.random.uniform(ks[7], (KG, D_INNER), f) * (math.log(0.1) - math.log(0.001)) + math.log(0.001))
        dt = jnp.clip(dt, 0.0001)
        dt_projs_bias = dt + jnp.log(-jnp.expm1(-dt))
        s = R_DT ** (-0.5)
        return {'x': jax.random.normal(ks[0], (B, D_MODEL, H, W), f), 'in_proj_w': jax.random.normal(ks[1], (2 * D_INNER, D_MODEL), f) * 0.02, 'off1_w': jax.random.normal(ks[2], (D_INNER, D_INNER, 3, 3), f) * 0.02, 'off1_b': jnp.zeros((D_INNER,), f), 'bn_gamma': jnp.ones((D_INNER,), f), 'bn_beta': jnp.zeros((D_INNER,), f), 'bn_mean': jnp.zeros((D_INNER,), f), 'bn_var': jnp.ones((D_INNER,), f), 'off2_w': jax.random.normal(ks[3], (2, D_INNER, 1, 1), f) * 0.02, 'x_proj_weight': jax.random.normal(ks[4], (KG, R_DT + 2 * N_STATE, D_INNER), f) * 0.02, 'dt_projs_weight': jax.random.uniform(ks[5], (KG, D_INNER, R_DT), f, -s, s), 'dt_projs_bias': dt_projs_bias, 'A_logs': jnp.log(jnp.tile(jnp.arange(1, N_STATE + 1, dtype=f), (KG * D_INNER, 1))), 'Ds': jnp.ones((KG * D_INNER,), f), 'ln_gamma': jnp.ones((D_INNER,), f), 'ln_beta': jnp.zeros((D_INNER,), f), 'out_proj_w': jax.random.normal(ks[6], (D_MODEL, D_INNER), f) * 0.02}
    _L0_conv_all = _L0_conv_setup()
    _L0_conv_in = {k: v for k, v in _L0_conv_all.items() if k in ('in_proj_w', 'off1_w', 'off1_b', 'bn_gamma', 'bn_beta', 'bn_mean', 'bn_var', 'off2_w', 'x_proj_weight', 'dt_projs_weight', 'dt_projs_bias', 'A_logs', 'Ds', 'ln_gamma', 'ln_beta', 'out_proj_w', )}
    del _L0_conv_all

    def _L1_conv_setup():
        import jax, jax.numpy as jnp
        import numpy as np
        DIM = 96
        D_STATE = 16
        D_CONV = 4
        EXPAND = 2
        D_INNER = EXPAND * DIM
        DT_RANK = (DIM + 15) // 16
        B, H, W = (4, 64, 64)

        def _mamba(u, in_proj_w, conv_w, conv_b, x_proj_w, dt_proj_w, dt_proj_b, A_log, Dp, out_proj_w):
            N, L, _ = u.shape
            xz = jnp.einsum('nld,ed->nle', u, in_proj_w)
            xs, z = jnp.split(xz, 2, axis=-1)
            xc = jax.lax.conv_general_dilated(xs.transpose(0, 2, 1), conv_w, (1,), [(D_CONV - 1, 0)], feature_group_count=D_INNER)
            xc = jax.nn.silu(xc + conv_b[None, :, None]).transpose(0, 2, 1)
            x_dbl = jnp.einsum('nld,ed->nle', xc, x_proj_w)
            dt, Bm, Cm = jnp.split(x_dbl, [DT_RANK, DT_RANK + D_STATE], axis=-1)
            delta = jax.nn.softplus(jnp.einsum('nlr,dr->nld', dt, dt_proj_w) + dt_proj_b)
            A = -jnp.exp(A_log)

            def step(h, inp):
                u_t, d_t, B_t, C_t = inp
                dA = jnp.exp(d_t[:, :, None] * A)
                h = dA * h + (d_t * u_t)[:, :, None] * B_t[:, None, :]
                y_t = jnp.einsum('nds,ns->nd', h, C_t)
                return (h, y_t)
            h0 = jnp.zeros((N, D_INNER, D_STATE), xc.dtype)
            xsw = (xc.transpose(1, 0, 2), delta.transpose(1, 0, 2), Bm.transpose(1, 0, 2), Cm.transpose(1, 0, 2))
            _, ys = jax.lax.scan(step, h0, xsw)
            y = ys.transpose(1, 0, 2) + xc * Dp
            y = y * jax.nn.silu(z)
            return jnp.einsum('nld,od->nlo', y, out_proj_w)
        key = jax.random.key(seed)
        ks = jax.random.split(key, 10)
        r = lambda k, shp, s=0.02: jax.random.normal(k, shp, jnp.float32) * s
        return {'x': jax.random.normal(ks[0], (B, DIM, H, W), jnp.float32), 'norm_g': jnp.ones((DIM,), jnp.float32), 'norm_b': jnp.zeros((DIM,), jnp.float32), 'gate_w1': r(ks[1], (DIM // 4, DIM)), 'gate_b1': jnp.zeros((DIM // 4,), jnp.float32), 'gate_w2': r(ks[2], (4, DIM // 4)), 'gate_b2': jnp.zeros((4,), jnp.float32), 'in_proj_w': r(ks[3], (2 * D_INNER, DIM)), 'conv_w': r(ks[4], (D_INNER, 1, D_CONV), 0.1), 'conv_b': jnp.zeros((D_INNER,), jnp.float32), 'x_proj_w': r(ks[5], (DT_RANK + 2 * D_STATE, D_INNER)), 'dt_proj_w': r(ks[6], (D_INNER, DT_RANK), 0.1), 'dt_proj_b': jnp.full((D_INNER,), -2.0, jnp.float32) + r(ks[7], (D_INNER,), 0.1), 'A_log': jnp.log(jnp.broadcast_to(jnp.arange(1, D_STATE + 1, dtype=jnp.float32), (D_INNER, D_STATE))), 'D': jnp.ones((D_INNER,), jnp.float32), 'out_proj_w': r(ks[8], (DIM, D_INNER))}
    _L1_conv_all = _L1_conv_setup()
    _L1_conv_in = {k: v for k, v in _L1_conv_all.items() if k in ('norm_g', 'norm_b', 'gate_w1', 'gate_b1', 'gate_w2', 'gate_b2', 'in_proj_w', 'conv_w', 'conv_b', 'x_proj_w', 'dt_proj_w', 'dt_proj_b', 'A_log', 'D', 'out_proj_w', )}
    del _L1_conv_all

    def _L2_conv_setup():
        import jax, jax.numpy as jnp
        from jax import lax
        import numpy as np
        D_MODEL = 96
        D_STATE = 16
        SSM_RATIO = 2.0
        D_CONV = 3
        K = 4
        D_INNER = int(SSM_RATIO * D_MODEL)
        DT_RANK = -(-D_MODEL // 16)
        B_SZ = 4
        H = 32
        W = 32

        def _snake_h(Hh, Ww):
            idx = np.tile(np.arange(Ww), (Hh, 1))
            idx[1::2] = idx[1::2, ::-1]
            return idx

        def _snake_v(Hh, Ww):
            idx = np.tile(np.arange(Hh)[:, None], (1, Ww))
            idx[:, 1::2] = idx[::-1, 1::2]
            return idx

        def _h_scan(x, d):
            Hh, Ww = x.shape[-2:]
            if d == 'left':
                x = jnp.flip(x, (-1, -2))
            return x[:, :, np.arange(Hh)[:, None], _snake_h(Hh, Ww)]

        def _v_scan(x, d):
            Bb, Cc, Hh, Ww = x.shape
            if d == 'up':
                x = jnp.flip(x, (-1, -2))
            t = x[:, :, _snake_v(Hh, Ww), np.arange(Ww)[None, :]]
            return jnp.swapaxes(t, -1, -2).reshape(Bb, Cc, Hh, Ww)

        def _h_merge(x, d):
            Hh, Ww = x.shape[-2:]
            t = x[:, :, np.arange(Hh)[:, None], _snake_h(Hh, Ww)]
            if d == 'left':
                t = jnp.flip(t, (-1, -2))
            return t

        def _v_merge(x, d):
            Hh, Ww = x.shape[-2:]
            t2 = jnp.swapaxes(x, -1, -2)
            t = t2[:, :, _snake_v(Hh, Ww), np.arange(Ww)[None, :]]
            if d == 'up':
                t = jnp.flip(t, (-1, -2))
            return t

        def cross_scan(x):
            return jnp.stack([_v_scan(x, 'down'), _v_scan(x, 'up'), _h_scan(x, 'right'), _h_scan(x, 'left')], axis=1)

        def cross_merge(ys):
            return _v_merge(ys[:, 0], 'down') + _v_merge(ys[:, 1], 'up') + _h_merge(ys[:, 2], 'right') + _h_merge(ys[:, 3], 'left')

        def selective_scan(u, delta, A, Bs, Cs, Dp, delta_bias):
            delta = jax.nn.softplus(delta + delta_bias[None, :, :, None])
            dA = jnp.exp(jnp.einsum('bkdl,kdn->lbkdn', delta, A))
            dBu = jnp.einsum('bkdl,bkdl,bknl->lbkdn', delta, u, Bs)
            Ct = jnp.moveaxis(Cs, -1, 0)

            def step(h, inp):
                dA_t, dBu_t, c_t = inp
                h = dA_t * h + dBu_t
                return (h, jnp.einsum('bkdn,bkn->bkd', h, c_t))
            h0 = jnp.zeros(dA.shape[1:], u.dtype)
            _, ys = lax.scan(step, h0, (dA, dBu, Ct))
            return jnp.moveaxis(ys, 0, -1) + Dp[None, :, :, None] * u
        key = jax.random.key(seed)
        ks = jax.random.split(key, 8)
        x = jax.random.normal(ks[0], (B_SZ, D_MODEL, H, W), jnp.float32)
        in_proj_w = jax.random.normal(ks[1], (2 * D_INNER, D_MODEL), jnp.float32) * D_MODEL ** (-0.5)
        conv_w = jax.random.normal(ks[2], (D_INNER, 1, D_CONV, D_CONV), jnp.float32) * 0.2
        conv_b = jnp.zeros((D_INNER,), jnp.float32)
        x_proj_w = jax.random.normal(ks[3], (K, DT_RANK + 2 * D_STATE, D_INNER), jnp.float32) * D_INNER ** (-0.5)
        s = DT_RANK ** (-0.5)
        dt_w = jax.random.uniform(ks[4], (K, D_INNER, DT_RANK), jnp.float32, -s, s)
        dt = jax.random.uniform(ks[5], (K, D_INNER), jnp.float32, 0.001, 0.1)
        dt_b = jnp.log(jnp.expm1(dt))
        A_logs = jnp.tile(jnp.log(jnp.arange(1, D_STATE + 1, dtype=jnp.float32)), (K * D_INNER, 1))
        Ds = jnp.ones((K * D_INNER,), jnp.float32)
        gn_gamma = jnp.ones((D_INNER,), jnp.float32)
        gn_beta = jnp.zeros((D_INNER,), jnp.float32)
        out_proj_w = jax.random.normal(ks[6], (D_MODEL, D_INNER), jnp.float32) * D_INNER ** (-0.5)
        return {'x': x, 'in_proj_w': in_proj_w, 'conv_w': conv_w, 'conv_b': conv_b, 'x_proj_w': x_proj_w, 'dt_w': dt_w, 'dt_b': dt_b, 'A_logs': A_logs, 'Ds': Ds, 'gn_gamma': gn_gamma, 'gn_beta': gn_beta, 'out_proj_w': out_proj_w}
    _L2_conv_all = _L2_conv_setup()
    _L2_conv_in = {k: v for k, v in _L2_conv_all.items() if k in ('in_proj_w', 'conv_w', 'conv_b', 'x_proj_w', 'dt_w', 'dt_b', 'A_logs', 'Ds', 'gn_gamma', 'gn_beta', 'out_proj_w', )}
    del _L2_conv_all

    def _L3_conv_setup():
        import jax, jax.numpy as jnp
        import jax.lax as lax
        import numpy as np
        D_MODEL, D_STATE, D_CONV, EXPAND = (96, 16, 3, 2)
        D_INNER = D_MODEL * EXPAND
        DT_RANK = max(1, D_MODEL // 16)
        N_DIRS = 4
        PROJ_DIM = DT_RANK + 2 * D_STATE
        LN_EPS = 1e-05

        def _combine(c1, c2):
            a1, b1 = c1
            a2, b2 = c2
            return (a1 * a2, a2 * b1 + b2)
        key = jax.random.key(seed)
        ks = jax.random.split(key, 8)
        B, H, W = (2, 56, 56)
        x = jax.random.normal(ks[0], (B, D_MODEL, H, W), dtype=jnp.float32)
        in_proj_w = jax.random.normal(ks[1], (D_MODEL, 2 * D_INNER), dtype=jnp.float32) * 0.02
        conv_w = jax.random.normal(ks[2], (D_INNER, 1, D_CONV, D_CONV), dtype=jnp.float32) * 0.1
        conv_b = jnp.zeros((D_INNER,), dtype=jnp.float32)
        x_proj_weight = jax.random.normal(ks[3], (N_DIRS, D_INNER, PROJ_DIM), dtype=jnp.float32) * 0.02
        dt_proj_weight = jax.random.normal(ks[4], (N_DIRS, D_INNER, DT_RANK), dtype=jnp.float32) * 0.02
        dt_proj_bias = jax.random.uniform(ks[5], (N_DIRS, D_INNER), dtype=jnp.float32) * 0.1
        A_log = jnp.broadcast_to(jnp.log(jnp.arange(1, D_STATE + 1, dtype=jnp.float32)), (D_INNER, D_STATE)).copy()
        D_skip = jnp.ones((D_INNER,), dtype=jnp.float32)
        ln_gamma = jnp.ones((D_INNER,), dtype=jnp.float32)
        ln_beta = jnp.zeros((D_INNER,), dtype=jnp.float32)
        out_proj_w = jax.random.normal(ks[6], (D_INNER, D_MODEL), dtype=jnp.float32) * 0.02
        return dict(x=x, in_proj_w=in_proj_w, conv_w=conv_w, conv_b=conv_b, x_proj_weight=x_proj_weight, dt_proj_weight=dt_proj_weight, dt_proj_bias=dt_proj_bias, A_log=A_log, D_skip=D_skip, ln_gamma=ln_gamma, ln_beta=ln_beta, out_proj_w=out_proj_w)
    _L3_conv_all = _L3_conv_setup()
    _L3_conv_in = {k: v for k, v in _L3_conv_all.items() if k in ('in_proj_w', 'conv_w', 'conv_b', 'x_proj_weight', 'dt_proj_weight', 'dt_proj_bias', 'A_log', 'D_skip', 'ln_gamma', 'ln_beta', 'out_proj_w', )}
    del _L3_conv_all

    return {
        "x": x,
        "L0_conv_in_proj_w": _L0_conv_in["in_proj_w"],
        "L0_conv_off1_w": _L0_conv_in["off1_w"],
        "L0_conv_off1_b": _L0_conv_in["off1_b"],
        "L0_conv_bn_gamma": _L0_conv_in["bn_gamma"],
        "L0_conv_bn_beta": _L0_conv_in["bn_beta"],
        "L0_conv_bn_mean": _L0_conv_in["bn_mean"],
        "L0_conv_bn_var": _L0_conv_in["bn_var"],
        "L0_conv_off2_w": _L0_conv_in["off2_w"],
        "L0_conv_x_proj_weight": _L0_conv_in["x_proj_weight"],
        "L0_conv_dt_projs_weight": _L0_conv_in["dt_projs_weight"],
        "L0_conv_dt_projs_bias": _L0_conv_in["dt_projs_bias"],
        "L0_conv_A_logs": _L0_conv_in["A_logs"],
        "L0_conv_Ds": _L0_conv_in["Ds"],
        "L0_conv_ln_gamma": _L0_conv_in["ln_gamma"],
        "L0_conv_ln_beta": _L0_conv_in["ln_beta"],
        "L0_conv_out_proj_w": _L0_conv_in["out_proj_w"],
        "L1_conv_norm_g": _L1_conv_in["norm_g"],
        "L1_conv_norm_b": _L1_conv_in["norm_b"],
        "L1_conv_gate_w1": _L1_conv_in["gate_w1"],
        "L1_conv_gate_b1": _L1_conv_in["gate_b1"],
        "L1_conv_gate_w2": _L1_conv_in["gate_w2"],
        "L1_conv_gate_b2": _L1_conv_in["gate_b2"],
        "L1_conv_in_proj_w": _L1_conv_in["in_proj_w"],
        "L1_conv_conv_w": _L1_conv_in["conv_w"],
        "L1_conv_conv_b": _L1_conv_in["conv_b"],
        "L1_conv_x_proj_w": _L1_conv_in["x_proj_w"],
        "L1_conv_dt_proj_w": _L1_conv_in["dt_proj_w"],
        "L1_conv_dt_proj_b": _L1_conv_in["dt_proj_b"],
        "L1_conv_A_log": _L1_conv_in["A_log"],
        "L1_conv_D": _L1_conv_in["D"],
        "L1_conv_out_proj_w": _L1_conv_in["out_proj_w"],
        "L2_conv_in_proj_w": _L2_conv_in["in_proj_w"],
        "L2_conv_conv_w": _L2_conv_in["conv_w"],
        "L2_conv_conv_b": _L2_conv_in["conv_b"],
        "L2_conv_x_proj_w": _L2_conv_in["x_proj_w"],
        "L2_conv_dt_w": _L2_conv_in["dt_w"],
        "L2_conv_dt_b": _L2_conv_in["dt_b"],
        "L2_conv_A_logs": _L2_conv_in["A_logs"],
        "L2_conv_Ds": _L2_conv_in["Ds"],
        "L2_conv_gn_gamma": _L2_conv_in["gn_gamma"],
        "L2_conv_gn_beta": _L2_conv_in["gn_beta"],
        "L2_conv_out_proj_w": _L2_conv_in["out_proj_w"],
        "L3_conv_in_proj_w": _L3_conv_in["in_proj_w"],
        "L3_conv_conv_w": _L3_conv_in["conv_w"],
        "L3_conv_conv_b": _L3_conv_in["conv_b"],
        "L3_conv_x_proj_weight": _L3_conv_in["x_proj_weight"],
        "L3_conv_dt_proj_weight": _L3_conv_in["dt_proj_weight"],
        "L3_conv_dt_proj_bias": _L3_conv_in["dt_proj_bias"],
        "L3_conv_A_log": _L3_conv_in["A_log"],
        "L3_conv_D_skip": _L3_conv_in["D_skip"],
        "L3_conv_ln_gamma": _L3_conv_in["ln_gamma"],
        "L3_conv_ln_beta": _L3_conv_in["ln_beta"],
        "L3_conv_out_proj_w": _L3_conv_in["out_proj_w"],
    }

def reference(x, L0_conv_in_proj_w, L0_conv_off1_w, L0_conv_off1_b, L0_conv_bn_gamma, L0_conv_bn_beta, L0_conv_bn_mean, L0_conv_bn_var, L0_conv_off2_w, L0_conv_x_proj_weight, L0_conv_dt_projs_weight, L0_conv_dt_projs_bias, L0_conv_A_logs, L0_conv_Ds, L0_conv_ln_gamma, L0_conv_ln_beta, L0_conv_out_proj_w, L1_conv_norm_g, L1_conv_norm_b, L1_conv_gate_w1, L1_conv_gate_b1, L1_conv_gate_w2, L1_conv_gate_b2, L1_conv_in_proj_w, L1_conv_conv_w, L1_conv_conv_b, L1_conv_x_proj_w, L1_conv_dt_proj_w, L1_conv_dt_proj_b, L1_conv_A_log, L1_conv_D, L1_conv_out_proj_w, L2_conv_in_proj_w, L2_conv_conv_w, L2_conv_conv_b, L2_conv_x_proj_w, L2_conv_dt_w, L2_conv_dt_b, L2_conv_A_logs, L2_conv_Ds, L2_conv_gn_gamma, L2_conv_gn_beta, L2_conv_out_proj_w, L3_conv_in_proj_w, L3_conv_conv_w, L3_conv_conv_b, L3_conv_x_proj_weight, L3_conv_dt_proj_weight, L3_conv_dt_proj_bias, L3_conv_A_log, L3_conv_D_skip, L3_conv_ln_gamma, L3_conv_ln_beta, L3_conv_out_proj_w):
    import jax
    import jax.numpy as jnp
    def _L0_conv_ref(x, in_proj_w, off1_w, off1_b, bn_gamma, bn_beta, bn_mean, bn_var, off2_w, x_proj_weight, dt_projs_weight, dt_projs_bias, A_logs, Ds, ln_gamma, ln_beta, out_proj_w):
        import jax, jax.numpy as jnp
        import numpy as np
        import math
        D_MODEL = 96
        SSM_RATIO = 2.0
        D_INNER = int(SSM_RATIO * D_MODEL)
        N_STATE = 16
        R_DT = math.ceil(D_MODEL / 16)
        KG = 4
        B, H, W = (2, 96, 96)
        KERNEL = 16

        def _conv(x, w, pad):
            return jax.lax.conv_general_dilated(x, w, (1, 1), [(pad, pad), (pad, pad)], dimension_numbers=('NCHW', 'OIHW', 'NCHW'))

        def grid_sample_bilinear(img, grid):
            Bb, C, Hh, Ww = img.shape
            gx = (grid[..., 0] + 1.0) * 0.5 * (Ww - 1)
            gy = (grid[..., 1] + 1.0) * 0.5 * (Hh - 1)
            x0 = jnp.floor(gx)
            y0 = jnp.floor(gy)
            x1 = x0 + 1.0
            y1 = y0 + 1.0
            bidx = jnp.arange(Bb)[:, None, None]

            def gather(yi, xi):
                valid = (yi >= 0) & (yi <= Hh - 1) & (xi >= 0) & (xi <= Ww - 1)
                yc = jnp.clip(yi, 0, Hh - 1).astype(jnp.int32)
                xc = jnp.clip(xi, 0, Ww - 1).astype(jnp.int32)
                v = img[bidx, :, yc, xc]
                return v * valid[..., None]
            wa = ((x1 - gx) * (y1 - gy))[..., None]
            wb = ((gx - x0) * (y1 - gy))[..., None]
            wc = ((x1 - gx) * (gy - y0))[..., None]
            wd = ((gx - x0) * (gy - y0))[..., None]
            out = gather(y0, x0) * wa + gather(y0, x1) * wb + gather(y1, x0) * wc + gather(y1, x1) * wd
            return jnp.moveaxis(out, -1, 1)

        def selective_scan(u, delta, A, Bm, Cm, Dv):
            Bt, K_, Dd, L = u.shape
            N = A.shape[-1]
            us = jnp.moveaxis(u, -1, 0)
            ds = jnp.moveaxis(delta, -1, 0)
            bs = jnp.moveaxis(Bm, -1, 0)
            cs = jnp.moveaxis(Cm, -1, 0)

            def step(hst, inputs):
                ut, dt, bt, ct = inputs
                dA = jnp.exp(dt[..., None] * A)
                hst = hst * dA + (dt * ut)[..., None] * bt[:, :, None, :]
                y = jnp.einsum('bkdn,bkn->bkd', hst, ct)
                return (hst, y)
            h0 = jnp.zeros((Bt, K_, Dd, N), u.dtype)
            _, ys = jax.lax.scan(step, h0, (us, ds, bs, cs))
            return jnp.moveaxis(ys, 0, -1) + Dv[None, :, :, None] * u
        Bb, Cm, Hh, Ww = x.shape
        d_inner = in_proj_w.shape[0] // 2
        xz = jnp.einsum('bchw,ec->behw', x, in_proj_w)
        xin, z = jnp.split(xz, 2, axis=1)
        z = jax.nn.silu(jnp.moveaxis(z, 1, -1))
        t = _conv(xin, off1_w, 1) + off1_b[None, :, None, None]
        t = (t - bn_mean[None, :, None, None]) * jax.lax.rsqrt(bn_var + 1e-05)[None, :, None, None]
        t = t * bn_gamma[None, :, None, None] + bn_beta[None, :, None, None]
        t = jax.nn.gelu(t, approximate=False)
        offset = _conv(t, off2_w, 0)
        orange = jnp.array([1.0 / (Hh - 1.0), 1.0 / (Ww - 1.0)], x.dtype)
        offset = jnp.tanh(offset) * orange[None, :, None, None]
        offset = jnp.moveaxis(offset, 1, -1)
        ry = jnp.linspace(0.5, Hh - 0.5, Hh) / (Hh - 1.0) * 2.0 - 1.0
        rx = jnp.linspace(0.5, Ww - 0.5, Ww) / (Ww - 1.0) * 2.0 - 1.0
        ref = jnp.stack(jnp.meshgrid(ry, rx, indexing='ij'), -1)
        pos = offset + ref[None]
        x_s = grid_sample_bilinear(xin, pos[..., ::-1])
        k = KERNEL
        h, w = (Hh // k, Ww // k)
        xt = x_s.reshape(Bb, d_inner, k, h, k, w).transpose(0, 2, 4, 1, 3, 5).reshape(Bb * k * k, d_inner, h, w)
        Bt = Bb * k * k
        L = h * w
        N = A_logs.shape[-1]
        R = dt_projs_weight.shape[-1]
        x_flat = xt.reshape(Bt, d_inner, L)
        x_wh = xt.transpose(0, 1, 3, 2).reshape(Bt, d_inner, L)
        x_hwwh = jnp.stack([x_flat, x_wh], axis=1)
        xs4 = jnp.concatenate([x_hwwh, x_hwwh[..., ::-1]], axis=1)
        x_dbl = jnp.einsum('bkdl,kcd->bkcl', xs4, x_proj_weight)
        dts = jnp.einsum('bkrl,kdr->bkdl', x_dbl[:, :, :R], dt_projs_weight)
        Bs = x_dbl[:, :, R:R + N]
        Cs = x_dbl[:, :, R + N:]
        delta = jax.nn.softplus(dts.astype(jnp.float32) + dt_projs_bias.astype(jnp.float32)[None, :, :, None])
        A = -jnp.exp(A_logs.astype(jnp.float32)).reshape(KG, d_inner, N)
        out_y = selective_scan(xs4.astype(jnp.float32), delta, A, Bs.astype(jnp.float32), Cs.astype(jnp.float32), Ds.astype(jnp.float32).reshape(KG, d_inner))
        inv_y = out_y[:, 2:4, :, ::-1]
        wh_y = out_y[:, 1].reshape(Bt, d_inner, w, h).transpose(0, 1, 3, 2).reshape(Bt, d_inner, L)
        invwh_y = inv_y[:, 1].reshape(Bt, d_inner, w, h).transpose(0, 1, 3, 2).reshape(Bt, d_inner, L)
        y = out_y[:, 0] + inv_y[:, 0] + wh_y + invwh_y
        y = y.transpose(0, 2, 1)
        mu = y.mean(-1, keepdims=True)
        var = ((y - mu) ** 2).mean(-1, keepdims=True)
        y = (y - mu) * jax.lax.rsqrt(var + 1e-05) * ln_gamma + ln_beta
        y = y.reshape(Bb, k, k, h, w, d_inner).transpose(0, 1, 3, 2, 4, 5).reshape(Bb, Hh, Ww, d_inner)
        y = y.astype(x.dtype) * z
        return jnp.einsum('bhwd,od->bohw', y, out_proj_w)

    def _L1_conv_ref(x, norm_g, norm_b, gate_w1, gate_b1, gate_w2, gate_b2, in_proj_w, conv_w, conv_b, x_proj_w, dt_proj_w, dt_proj_b, A_log, D, out_proj_w):
        import jax, jax.numpy as jnp
        import numpy as np
        DIM = 96
        D_STATE = 16
        D_CONV = 4
        EXPAND = 2
        D_INNER = EXPAND * DIM
        DT_RANK = (DIM + 15) // 16
        B, H, W = (4, 64, 64)

        def _mamba(u, in_proj_w, conv_w, conv_b, x_proj_w, dt_proj_w, dt_proj_b, A_log, Dp, out_proj_w):
            N, L, _ = u.shape
            xz = jnp.einsum('nld,ed->nle', u, in_proj_w)
            xs, z = jnp.split(xz, 2, axis=-1)
            xc = jax.lax.conv_general_dilated(xs.transpose(0, 2, 1), conv_w, (1,), [(D_CONV - 1, 0)], feature_group_count=D_INNER)
            xc = jax.nn.silu(xc + conv_b[None, :, None]).transpose(0, 2, 1)
            x_dbl = jnp.einsum('nld,ed->nle', xc, x_proj_w)
            dt, Bm, Cm = jnp.split(x_dbl, [DT_RANK, DT_RANK + D_STATE], axis=-1)
            delta = jax.nn.softplus(jnp.einsum('nlr,dr->nld', dt, dt_proj_w) + dt_proj_b)
            A = -jnp.exp(A_log)

            def step(h, inp):
                u_t, d_t, B_t, C_t = inp
                dA = jnp.exp(d_t[:, :, None] * A)
                h = dA * h + (d_t * u_t)[:, :, None] * B_t[:, None, :]
                y_t = jnp.einsum('nds,ns->nd', h, C_t)
                return (h, y_t)
            h0 = jnp.zeros((N, D_INNER, D_STATE), xc.dtype)
            xsw = (xc.transpose(1, 0, 2), delta.transpose(1, 0, 2), Bm.transpose(1, 0, 2), Cm.transpose(1, 0, 2))
            _, ys = jax.lax.scan(step, h0, xsw)
            y = ys.transpose(1, 0, 2) + xc * Dp
            y = y * jax.nn.silu(z)
            return jnp.einsum('nld,od->nlo', y, out_proj_w)
        Bb, C, Hh, Ww = x.shape
        L = Hh * Ww
        xp = x.transpose(0, 2, 3, 1)
        mu = xp.mean(-1, keepdims=True)
        var = xp.var(-1, keepdims=True)
        xn = (xp - mu) * jax.lax.rsqrt(var + 1e-05) * norm_g + norm_b
        gate = jax.nn.softmax(jnp.tanh(xn @ gate_w1.T + gate_b1) @ gate_w2.T + gate_b2, axis=-1)
        xcln = xn.transpose(0, 3, 1, 2)
        x_hw = xcln.reshape(Bb, C, L).transpose(0, 2, 1)
        x_wh = xcln.transpose(0, 1, 3, 2).reshape(Bb, C, L).transpose(0, 2, 1)
        seqs = jnp.concatenate([x_hw, x_wh, x_hw[:, ::-1], x_wh[:, ::-1]], axis=0)
        outs = _mamba(seqs, in_proj_w, conv_w, conv_b, x_proj_w, dt_proj_w, dt_proj_b, A_log, D, out_proj_w)
        o1, o2, o3, o4 = jnp.split(outs, 4, axis=0)
        y1 = o1.transpose(0, 2, 1).reshape(Bb, C, Hh, Ww)
        y2 = o2.transpose(0, 2, 1).reshape(Bb, C, Ww, Hh).transpose(0, 1, 3, 2)
        y3 = o3[:, ::-1].transpose(0, 2, 1).reshape(Bb, C, Hh, Ww)
        y4 = o4[:, ::-1].transpose(0, 2, 1).reshape(Bb, C, Ww, Hh).transpose(0, 1, 3, 2)
        ys = jnp.stack([y1, y2, y3, y4], axis=-1).transpose(0, 2, 3, 1, 4)
        yf = (ys * gate[:, :, :, None, :]).sum(-1)
        return yf.transpose(0, 3, 1, 2)

    def _L2_conv_ref(x, in_proj_w, conv_w, conv_b, x_proj_w, dt_w, dt_b, A_logs, Ds, gn_gamma, gn_beta, out_proj_w):
        import jax, jax.numpy as jnp
        from jax import lax
        import numpy as np
        D_MODEL = 96
        D_STATE = 16
        SSM_RATIO = 2.0
        D_CONV = 3
        K = 4
        D_INNER = int(SSM_RATIO * D_MODEL)
        DT_RANK = -(-D_MODEL // 16)
        B_SZ = 4
        H = 32
        W = 32

        def _snake_h(Hh, Ww):
            idx = np.tile(np.arange(Ww), (Hh, 1))
            idx[1::2] = idx[1::2, ::-1]
            return idx

        def _snake_v(Hh, Ww):
            idx = np.tile(np.arange(Hh)[:, None], (1, Ww))
            idx[:, 1::2] = idx[::-1, 1::2]
            return idx

        def _h_scan(x, d):
            Hh, Ww = x.shape[-2:]
            if d == 'left':
                x = jnp.flip(x, (-1, -2))
            return x[:, :, np.arange(Hh)[:, None], _snake_h(Hh, Ww)]

        def _v_scan(x, d):
            Bb, Cc, Hh, Ww = x.shape
            if d == 'up':
                x = jnp.flip(x, (-1, -2))
            t = x[:, :, _snake_v(Hh, Ww), np.arange(Ww)[None, :]]
            return jnp.swapaxes(t, -1, -2).reshape(Bb, Cc, Hh, Ww)

        def _h_merge(x, d):
            Hh, Ww = x.shape[-2:]
            t = x[:, :, np.arange(Hh)[:, None], _snake_h(Hh, Ww)]
            if d == 'left':
                t = jnp.flip(t, (-1, -2))
            return t

        def _v_merge(x, d):
            Hh, Ww = x.shape[-2:]
            t2 = jnp.swapaxes(x, -1, -2)
            t = t2[:, :, _snake_v(Hh, Ww), np.arange(Ww)[None, :]]
            if d == 'up':
                t = jnp.flip(t, (-1, -2))
            return t

        def cross_scan(x):
            return jnp.stack([_v_scan(x, 'down'), _v_scan(x, 'up'), _h_scan(x, 'right'), _h_scan(x, 'left')], axis=1)

        def cross_merge(ys):
            return _v_merge(ys[:, 0], 'down') + _v_merge(ys[:, 1], 'up') + _h_merge(ys[:, 2], 'right') + _h_merge(ys[:, 3], 'left')

        def selective_scan(u, delta, A, Bs, Cs, Dp, delta_bias):
            delta = jax.nn.softplus(delta + delta_bias[None, :, :, None])
            dA = jnp.exp(jnp.einsum('bkdl,kdn->lbkdn', delta, A))
            dBu = jnp.einsum('bkdl,bkdl,bknl->lbkdn', delta, u, Bs)
            Ct = jnp.moveaxis(Cs, -1, 0)

            def step(h, inp):
                dA_t, dBu_t, c_t = inp
                h = dA_t * h + dBu_t
                return (h, jnp.einsum('bkdn,bkn->bkd', h, c_t))
            h0 = jnp.zeros(dA.shape[1:], u.dtype)
            _, ys = lax.scan(step, h0, (dA, dBu, Ct))
            return jnp.moveaxis(ys, 0, -1) + Dp[None, :, :, None] * u
        Bb, _, Hh, Ww = x.shape
        L = Hh * Ww
        xz = jnp.einsum('bchw,oc->bohw', x, in_proj_w)
        xx, z = jnp.split(xz, 2, axis=1)
        z = jax.nn.silu(z)
        xx = lax.conv_general_dilated(xx, conv_w, (1, 1), 'SAME', feature_group_count=D_INNER, dimension_numbers=('NCHW', 'OIHW', 'NCHW')) + conv_b[None, :, None, None]
        xx = jax.nn.silu(xx)
        xs = cross_scan(xx).reshape(Bb, K, D_INNER, L)
        x_dbl = jnp.einsum('bkdl,kcd->bkcl', xs, x_proj_w)
        dts = jnp.einsum('bkrl,kdr->bkdl', x_dbl[:, :, :DT_RANK], dt_w)
        Bs = x_dbl[:, :, DT_RANK:DT_RANK + D_STATE]
        Cs = x_dbl[:, :, DT_RANK + D_STATE:]
        A = -jnp.exp(A_logs).reshape(K, D_INNER, D_STATE)
        y = selective_scan(xs, dts, A, Bs, Cs, Ds.reshape(K, D_INNER), dt_b)
        y = cross_merge(y.reshape(Bb, K, D_INNER, Hh, Ww))
        mu = jnp.mean(y, axis=(1, 2, 3), keepdims=True)
        var = jnp.var(y, axis=(1, 2, 3), keepdims=True)
        y = (y - mu) * lax.rsqrt(var + 1e-06)
        y = y * gn_gamma[None, :, None, None] + gn_beta[None, :, None, None]
        y = y * z
        return jnp.einsum('bchw,oc->bohw', y, out_proj_w)

    def _L3_conv_ref(x, in_proj_w, conv_w, conv_b, x_proj_weight, dt_proj_weight, dt_proj_bias, A_log, D_skip, ln_gamma, ln_beta, out_proj_w):
        import jax, jax.numpy as jnp
        import jax.lax as lax
        import numpy as np
        D_MODEL, D_STATE, D_CONV, EXPAND = (96, 16, 3, 2)
        D_INNER = D_MODEL * EXPAND
        DT_RANK = max(1, D_MODEL // 16)
        N_DIRS = 4
        PROJ_DIM = DT_RANK + 2 * D_STATE
        LN_EPS = 1e-05

        def _combine(c1, c2):
            a1, b1 = c1
            a2, b2 = c2
            return (a1 * a2, a2 * b1 + b2)
        B, D, H, W = x.shape
        E, N, R = (D_INNER, D_STATE, DT_RANK)
        L = H * W
        x_flat = x.reshape(B, D, L).transpose(0, 2, 1)
        xz = x_flat @ in_proj_w
        xb, z = (xz[..., :E], xz[..., E:])
        xb = xb.transpose(0, 2, 1).reshape(B, E, H, W)
        xb = lax.conv_general_dilated(xb, conv_w, (1, 1), 'SAME', feature_group_count=E, dimension_numbers=('NCHW', 'OIHW', 'NCHW'))
        xb = jax.nn.silu(xb + conv_b[None, :, None, None])
        x_rm = xb.reshape(B, E, L)
        x_cm = xb.transpose(0, 1, 3, 2).reshape(B, E, L)
        xs = jnp.stack([x_rm, x_rm[..., ::-1], x_cm, x_cm[..., ::-1]], axis=0)
        x_dbl = jnp.einsum('kbel,ker->kblr', xs, x_proj_weight)
        dt_r = x_dbl[..., :R]
        Bs = x_dbl[..., R:R + N]
        Cs = x_dbl[..., R + N:]
        dt = jnp.einsum('kblr,ker->kbel', dt_r, dt_proj_weight) + dt_proj_bias[:, None, :, None]
        dt = jax.nn.softplus(dt)
        A = -jnp.exp(A_log)
        deltaA = jnp.exp(dt[..., None] * A[None, None, :, None, :])
        deltaBx = (dt * xs)[..., None] * Bs[:, :, None, :, :]
        _, h = lax.associative_scan(_combine, (deltaA, deltaBx), axis=3)
        ys = jnp.einsum('kbeln,kbln->kbel', h, Cs) + xs * D_skip[None, None, :, None]
        ys = ys.at[1].set(ys[1][..., ::-1]).at[3].set(ys[3][..., ::-1])
        y_row = (ys[0] + ys[1]).reshape(B, E, H, W)
        y_col = (ys[2] + ys[3]).reshape(B, E, W, H).transpose(0, 1, 3, 2)
        y = (y_row + y_col).reshape(B, E, L).transpose(0, 2, 1)
        mu = jnp.mean(y, axis=-1, keepdims=True)
        var = jnp.var(y, axis=-1, keepdims=True)
        y = (y - mu) * lax.rsqrt(var + LN_EPS) * ln_gamma + ln_beta
        y = y * jax.nn.silu(z)
        y = y @ out_proj_w
        return y.transpose(0, 2, 1).reshape(B, D, H, W)

    def _gn(v, G=32, eps=1e-5):
        B_, C_, H_, W_ = v.shape
        g = v.reshape(B_, G, C_ // G, H_, W_)
        m = jnp.mean(g, axis=(2, 3, 4), keepdims=True)
        s = jnp.var(g, axis=(2, 3, 4), keepdims=True)
        return ((g - m) / jnp.sqrt(s + eps)).reshape(v.shape)

    def _ln_c(v, eps=1e-6):
        m = jnp.mean(v, axis=1, keepdims=True)
        s = jnp.var(v, axis=1, keepdims=True)
        return (v - m) / jnp.sqrt(s + eps)

    def _ln_t(v, eps=1e-5):
        m = jnp.mean(v, axis=-1, keepdims=True)
        s = jnp.var(v, axis=-1, keepdims=True)
        return (v - m) / jnp.sqrt(s + eps)

    def _to_tokens(v):
        B_, C_, H_, W_ = v.shape
        return v.reshape(B_, C_, H_ * W_).transpose(0, 2, 1)
    def _from_tokens(t, like):
        B_, C_, H_, W_ = like.shape
        return t.transpose(0, 2, 1).reshape(B_, C_, H_, W_)

    x = x + _L0_conv_ref(_gn(x), L0_conv_in_proj_w, L0_conv_off1_w, L0_conv_off1_b, L0_conv_bn_gamma, L0_conv_bn_beta, L0_conv_bn_mean, L0_conv_bn_var, L0_conv_off2_w, L0_conv_x_proj_weight, L0_conv_dt_projs_weight, L0_conv_dt_projs_bias, L0_conv_A_logs, L0_conv_Ds, L0_conv_ln_gamma, L0_conv_ln_beta, L0_conv_out_proj_w)
    x = x + _L1_conv_ref(_gn(x), L1_conv_norm_g, L1_conv_norm_b, L1_conv_gate_w1, L1_conv_gate_b1, L1_conv_gate_w2, L1_conv_gate_b2, L1_conv_in_proj_w, L1_conv_conv_w, L1_conv_conv_b, L1_conv_x_proj_w, L1_conv_dt_proj_w, L1_conv_dt_proj_b, L1_conv_A_log, L1_conv_D, L1_conv_out_proj_w)
    x = x + _L2_conv_ref(_gn(x), L2_conv_in_proj_w, L2_conv_conv_w, L2_conv_conv_b, L2_conv_x_proj_w, L2_conv_dt_w, L2_conv_dt_b, L2_conv_A_logs, L2_conv_Ds, L2_conv_gn_gamma, L2_conv_gn_beta, L2_conv_out_proj_w)
    x = x + _L3_conv_ref(_gn(x), L3_conv_in_proj_w, L3_conv_conv_w, L3_conv_conv_b, L3_conv_x_proj_weight, L3_conv_dt_proj_weight, L3_conv_dt_proj_bias, L3_conv_A_log, L3_conv_D_skip, L3_conv_ln_gamma, L3_conv_ln_beta, L3_conv_out_proj_w)
    return x


_drawn_inputs = setup_inputs


def setup_inputs(seed=0):
    import zlib

    import numpy as np

    out = dict(_drawn_inputs(seed))
    spreads = {'L0_conv_off1_b': (0.0, 0.1),
     'L0_conv_bn_gamma': (1.0, 0.2),
     'L0_conv_bn_beta': (0.0, 0.1),
     'L0_conv_bn_mean': (0.0, 0.1),
     'L0_conv_bn_var': (1.0, 0.2),
     'L0_conv_Ds': (1.0, 0.2),
     'L0_conv_ln_gamma': (1.0, 0.2),
     'L0_conv_ln_beta': (0.0, 0.1),
     'L1_conv_norm_g': (1.0, 0.2),
     'L1_conv_norm_b': (0.0, 0.1),
     'L1_conv_gate_b1': (0.0, 0.1),
     'L1_conv_gate_b2': (0.0, 0.1),
     'L1_conv_conv_b': (0.0, 0.1),
     'L1_conv_D': (1.0, 0.2),
     'L2_conv_conv_b': (0.0, 0.1),
     'L2_conv_Ds': (1.0, 0.2),
     'L2_conv_gn_gamma': (1.0, 0.2),
     'L2_conv_gn_beta': (0.0, 0.1),
     'L3_conv_conv_b': (0.0, 0.1),
     'L3_conv_D_skip': (1.0, 0.2),
     'L3_conv_ln_gamma': (1.0, 0.2),
     'L3_conv_ln_beta': (0.0, 0.1)}
    factors = {}
    for name, (base, spread) in spreads.items():
        noise = np.random.default_rng([zlib.crc32(name.encode()), seed]).standard_normal(out[name].shape)
        drawn = base * np.exp(spread * noise) if base else spread * noise
        out[name] = jnp.asarray(drawn.astype(out[name].dtype))
    for name, factor in factors.items():
        out[name] = (out[name] * factor).astype(out[name].dtype)
    return out
```

```python
from contextlib import ExitStack

import numpy as np

import concourse.bass as bass
from concourse import mybir

F32 = mybir.dt.float32
BF16 = mybir.dt.bfloat16
U16 = mybir.dt.uint16
ALU = mybir.AluOpType
ACT = mybir.ActivationFunctionType

P = 128
IMAGES = 2
CH = 96
HID = 192
TILES = 3
STATES = 16
RANK = 6
DIRS = 4
SIDE = 96
PADDED = SIDE + 2
L = SIDE * SIDE
GROUP = 3
KERNEL = 6
WINDOW = KERNEL * KERNEL
GATE_HID = CH // 4
TAPS = 9
SEQ_TAPS = 4
BC_ROWS = 2 * IMAGES * STATES
DBL_ROWS = BC_ROWS + IMAGES * RANK
PARTS = 3
ONE = 1
RESET_DELTA = 1.0e30


class Phase:

    def __init__(self, nc, name):
        self.nc, self.name, self.stack, self.sems, self.fresh = nc, name, ExitStack(), [], []

    def __enter__(self):
        return self

    def __exit__(self, *exc):
        for s in self.sems:
            self.nc.gpsimd.sem_clear(s)
        self.nc.all_engine_barrier()
        self.stack.close()

    def sb(self, name, shape, dt=F32):
        return self.stack.enter_context(self.nc.sbuf_tensor(f"{self.name}_{name}", shape, dt))

    def ps(self, name, shape, dt=F32):
        return self.stack.enter_context(self.nc.psum_tensor(f"{self.name}_{name}", shape, dt))

    def sem(self, name):
        self.sems.append(self.stack.enter_context(self.nc.semaphore(f"{self.name}_{name}")))
        self.fresh.append(self.sems[-1])
        return self.sems[-1]

    def block(self):
        for s in self.fresh:
            self.nc.gpsimd.sem_inc(s, ONE)
        self.fresh = []
        self.nc.all_engine_barrier()
        return self.nc.Block()


WALKS = {
    0: [("window", False, "row"), ("window", False, "col"), ("window", True, "row"), ("window", True, "col")],
    1: [("row", False, "up"), ("col", False, "up"), ("row", True, "down"), ("col", True, "down")],
    2: [("col", False, "snake"), ("col", True, "snake"), ("row", False, "snake"), ("row", True, "snake")],
    3: [("row", False, "up"), ("row", True, "down"), ("col", False, "up"), ("col", True, "down")],
}
MAJORS = 12
CHUNK = MAJORS * SIDE
CHUNKS = L // CHUNK
SUB = CHUNK // 3


def walk_pairs(walk, c, grid, seq):
    axis, down, minor = walk
    if axis == "window":
        pairs = []
        n = SIDE * KERNEL
        for s in range(MAJORS // KERNEL):
            if down:
                first = c * (-MAJORS) + (SIDE - KERNEL * (s + 1))
            else:
                first = c * MAJORS + KERNEL * s
            win = grid[:, bass.ds(first, KERNEL), :].rearrange("p r (w c) -> p w r c", c=KERNEL)
            if minor == "col":
                win = win.rearrange("p w r c -> p w c r")
            line = seq[:, s * n:(s + 1) * n].rearrange("p (w r c) -> p w r c", r=KERNEL, c=KERNEL)
            if down:
                line = line[:, ::-1, ::-1, ::-1]
            pairs.append((win, line))
        return pairs
    first = c * (-MAJORS) + (SIDE - MAJORS) if down else c * MAJORS
    if axis == "row":
        block = grid[:, bass.ds(first, MAJORS), :]
    else:
        block = grid[:, :, bass.ds(first, MAJORS)].rearrange("p r c -> p c r")
    line = seq.rearrange("p (m n) -> p m n", n=SIDE)
    if down:
        line = line[:, ::-1, :]
    if minor == "up":
        return [(block, line)]
    if minor == "down":
        return [(block, line[:, :, ::-1])]
    return [(block[:, 0::2, :], line[:, 0::2, :]), (block[:, 1::2, :], line[:, 1::2, ::-1])]


def norm_gate(nc, x_d, w, out_d, gate_d):
    with Phase(nc, "ng") as ph:
        x, scale, bias, loaded, stats = group_norm_head(nc, ph, x_d, w)
        N = SUB
        STEPS = L // N
        mean96 = ph.sb("mean96", [CH, CH])
        w1 = ph.sb("w1", [CH, GATE_HID])
        w2 = ph.sb("w2", [GATE_HID, DIRS])
        vecs = ph.sb("vecs", [CH, 2])
        b1 = ph.sb("b1", [GATE_HID, 1])
        b2 = ph.sb("b2", [P, DIRS])
        eye = ph.sb("eye", [P, P])
        xn = ph.sb("xn", [CH, N])
        xc = ph.sb("xc", [CH, N])
        sq = ph.sb("sq", [CH, N])
        sd = ph.sb("sd", [CH, N])
        rs = ph.sb("rs", [CH, N])
        xl = ph.sb("xl", [CH, 2, N])
        th = ph.sb("th", [GATE_HID, N])
        lg = ph.sb("lg", [P, 3, DIRS])
        mx = ph.sb("mx", [P, 3])
        sm = ph.sb("sm", [P, 3])
        gt = ph.sb("gt", [DIRS, 2, N])
        p_mean = ph.ps("p_mean", [CH, 512])
        p_var = ph.ps("p_var", [CH, 512])
        p_hid = ph.ps("p_hid", [GATE_HID, 512])
        p_log = ph.ps("p_log", [P, 3, DIRS])
        p_gt = ph.ps("p_gt", [DIRS, 512])
        weights = ph.sem("weights")
        eps_ready = ph.sem("eps_ready")
        act = ph.sem("act")
        dve = ph.sem("dve")
        pe = ph.sem("pe")
        xl_stored = [ph.sem(f"xl_stored{b}") for b in range(IMAGES)]
        gt_stored = [ph.sem(f"gt_stored{b}") for b in range(IMAGES)]
        A, D, E = 6, 13, 5
        eps = ph.sb("eps", [CH, 1])

        block_cm = ph.block()
        block = block_cm.__enter__()

        @block.sync
        def _(sp):
            for dst, src in ((mean96, w["mean96"]), (w1, w["gate_w1"]), (w2, w["gate_w2"]), (vecs, w["norm_gb"]),
                             (b1, w["gate_b1"]), (b2, w["gate_b2"]), (eye, w["eye"])):
                sp.dma_start(dst[:], src).then_inc(weights, 16)
            with sp.Fori(0, STEPS) as i:
                for b in range(IMAGES):
                    sp.wait_ge(act, i * (2 * A) + (b * A + 4) + ONE)
                    sp.dma_start(out_d[b, :, bass.ds(i * N, N)], xl[:, b, :]).then_inc(xl_stored[b], 16)
                    sp.wait_ge(dve, i * (2 * D) + (b * D + D) + ONE)
                    sp.dma_start(gate_d[b * DIRS:(b + 1) * DIRS, bass.ds(i * N, N)], gt[:, b, :]).then_inc(gt_stored[b], 16)
            for b in range(IMAGES):
                sp.wait_ge(xl_stored[b], 16 * STEPS + ONE)
                sp.wait_ge(gt_stored[b], 16 * STEPS + ONE)

        @block.scalar
        def _(a):
            a.wait_ge(weights, 16 * 7 + ONE)
            a.wait_ge(eps_ready, 1 + ONE)
            with a.Fori(0, STEPS) as i:
                for b in range(IMAGES):
                    s, v = i * (2 * A) + b * A, i * (2 * D) + b * D
                    q = i * (2 * E) + b * E
                    a.wait_ge(dve, v + ONE)
                    nc.scalar.activation(xn[:], x[:, b, bass.ds(i * N, N)], ACT.Identity, bias=bias[:, b:b + 1],
                                         scale=scale[:, b:b + 1]).then_inc(act, 1)
                    a.wait_ge(dve, v + 1 + ONE)
                    nc.scalar.activation(sq[:], xc[:], ACT.Square).then_inc(act, 1)
                    a.wait_ge(pe, q + 2 + ONE)
                    nc.scalar.activation(sd[:], p_var[:, 0:N], ACT.Sqrt, bias=eps[:]).then_inc(act, 1)
                    a.wait_ge(dve, v + 3 + ONE)
                    a.wait_ge(xl_stored[b], i * 16 + ONE)
                    nc.scalar.activation(xl[:, b, :], xc[:], ACT.Identity, bias=vecs[:, 1:2], scale=vecs[:, 0:1]).then_inc(act, 1)
                    a.wait_ge(pe, q + 3 + ONE)
                    nc.scalar.activation(th[:], p_hid[:, 0:N], ACT.Tanh, bias=b1[:]).then_inc(act, 1)
                    a.wait_ge(dve, v + 8 + ONE)
                    nc.scalar.activation(lg[:], lg[:], ACT.Exp).then_inc(act, 1)

        @block.tensor
        def _(t):
            t.wait_ge(weights, 16 * 7 + ONE)
            with t.Fori(0, STEPS) as i:
                for b in range(IMAGES):
                    s, v = i * (2 * A) + b * A, i * (2 * D) + b * D
                    t.wait_ge(act, s + 1 + ONE)
                    nc.tensor.matmul(p_mean[:, 0:N], mean96[:], xn[:], start=True, stop=True).then_inc(pe, 1)
                    t.wait_ge(act, s + 2 + ONE)
                    nc.tensor.matmul(p_var[:, 0:N], mean96[:], sq[:], start=True, stop=True).then_inc(pe, 1)
                    t.wait_ge(act, s + 4 + ONE)
                    nc.tensor.matmul(p_hid[:, 0:N], w1[:], xl[:, b, :], start=True, stop=True).then_inc(pe, 1)
                    t.wait_ge(act, s + 5 + ONE)
                    for m in range(3):
                        last = nc.tensor.matmul(p_log[:, m, :], th[:, m * P:(m + 1) * P], w2[:], start=True, stop=True)
                    last.then_inc(pe, 1)
                    t.wait_ge(dve, v + 12 + ONE)
                    for m in range(3):
                        last = nc.tensor.transpose(p_gt[:, m * P:(m + 1) * P], lg[:, m, :], eye[:])
                    last.then_inc(pe, 1)

        @block.vector
        def _(d):
            nc.vector.memset(eps[:], 1e-5).then_inc(eps_ready, 1)
            d.wait_ge(weights, 16 * 7 + ONE)
            with d.Fori(0, STEPS) as i:
                for b in range(IMAGES):
                    s, v = i * (2 * A) + b * A, i * (2 * D) + b * D
                    q = i * (2 * E) + b * E

                    d.wait_ge(pe, q + 1 + ONE)
                    nc.vector.tensor_tensor(xc[:], xn[:], p_mean[:, 0:N], ALU.subtract).then_inc(dve, 1)
                    d.wait_ge(act, s + 3 + ONE)
                    nc.vector.reciprocal(rs[:], sd[:]).then_inc(dve, 1)
                    d.wait_ge(dve, v + 2 + ONE)
                    nc.vector.tensor_tensor(xc[:], xc[:], rs[:], ALU.mult).then_inc(dve, 1)
                    d.wait_ge(pe, q + 4 + ONE)
                    nc.vector.tensor_tensor(lg[:], p_log[:], b2[:].unsqueeze(1).broadcast_to([P, 3, DIRS]), ALU.add).then_inc(dve, 1)
                    d.wait_ge(dve, v + 4 + ONE)
                    nc.vector.tensor_reduce(mx[:], lg[:], mybir.AxisListType.X, ALU.max).then_inc(dve, 1)
                    for k in range(3):
                        d.wait_ge(dve, v + 5 + ONE)
                        nc.vector.tensor_scalar(lg[:, k, :], lg[:, k, :], mx[:, k:k + 1], None, ALU.subtract).then_inc(dve, 1)
                    d.wait_ge(act, s + 6 + ONE)
                    nc.vector.tensor_reduce(sm[:], lg[:], mybir.AxisListType.X, ALU.add).then_inc(dve, 1)
                    d.wait_ge(dve, v + 9 + ONE)
                    nc.vector.reciprocal(mx[:], sm[:]).then_inc(dve, 1)
                    d.wait_ge(dve, v + 10 + ONE)
                    nc.vector.tensor_tensor(lg[:, 0:2, :], lg[:, 0:2, :], mx[:, 0:2].unsqueeze(2).broadcast_to([P, 2, DIRS]), ALU.mult).then_inc(dve, 1)
                    nc.vector.tensor_tensor(lg[:, 2:3, :], lg[:, 2:3, :], mx[:, 2:3].unsqueeze(2).broadcast_to([P, 1, DIRS]), ALU.mult).then_inc(dve, 1)
                    d.wait_ge(pe, q + 5 + ONE)
                    d.wait_ge(gt_stored[b], i * 16 + ONE)
                    nc.vector.tensor_copy(gt[:, b, :], p_gt[:, 0:N]).then_inc(dve, 1)

        block_cm.__exit__(None, None, None)


def group_norm_head(nc, ph, x_d, w):
    x = ph.sb("x", [CH, IMAGES, L])
    avg = ph.sb("avg", [CH, CH])
    BN = 512
    NBN = L // BN
    bn = ph.sb("bn", [CH, IMAGES, NBN, 6])
    mv = ph.sb("mv", [CH, IMAGES, 2])
    sq = ph.sb("gsq", [CH, IMAGES])
    scale = ph.sb("scale", [CH, IMAGES])
    bias = ph.sb("gbias", [CH, IMAGES])
    var = ph.sb("gvar", [CH, IMAGES])
    eps5 = ph.sb("eps5", [CH, 1])
    loaded = ph.sem("x_loaded")
    stats = ph.sem("x_stats")
    dev = ph.sem("x_dev")
    with ExitStack() as st:
        pg = st.enter_context(nc.psum_tensor(f"{ph.name}_pg", [CH, IMAGES * 2], F32))
        with ph.block() as block:
            @block.sync
            def _(sp):
                sp.dma_start(avg[:], w["avg"]).then_inc(loaded, 16)
                for b in range(IMAGES):
                    for h in range(2):
                        sp.dma_start(x[:, b, h * L // 2:(h + 1) * L // 2], x_d[b, :, h * L // 2:(h + 1) * L // 2]).then_inc(loaded, 16)

            @block.vector
            def _(d):
                nc.vector.memset(eps5[:], 1e-5).then_inc(stats, 1)
                for b in range(IMAGES):
                    for n in range(NBN):
                        d.wait_ge(loaded, 16 * 5 + ONE)
                        nc.vector.bn_stats(bn[:, b, n, :], x[:, b, n * BN:(n + 1) * BN]).then_inc(stats, 1)
                k = 1 + IMAGES * NBN
                d.wait_ge(stats, k + ONE)
                for b in range(IMAGES):
                    nc.vector.bn_aggr(mv[:, b, :], bn[:, b, :, :].rearrange("p n s -> p (n s)")).then_inc(stats, 1)
                k += IMAGES
                d.wait_ge(stats, k + ONE)
                nc.vector.tensor_tensor(sq[:], mv[:, :, 0], mv[:, :, 0], ALU.mult).then_inc(stats, 1)
                d.wait_ge(stats, k + 1 + ONE)
                nc.vector.tensor_tensor(mv[:, :, 1], mv[:, :, 1], sq[:], ALU.add).then_inc(stats, 1)
                d.wait_ge(stats, k + 3 + ONE)
                nc.vector.tensor_copy(mv[:].rearrange("p b s -> p (b s)"), pg[:]).then_inc(stats, 1)
                d.wait_ge(stats, k + 4 + ONE)
                nc.vector.tensor_tensor(sq[:], mv[:, :, 0], mv[:, :, 0], ALU.mult).then_inc(stats, 1)
                d.wait_ge(stats, k + 5 + ONE)
                nc.vector.tensor_tensor(var[:], mv[:, :, 1], sq[:], ALU.subtract).then_inc(stats, 1)
                d.wait_ge(dev, 1 + ONE)
                nc.vector.reciprocal(scale[:], sq[:]).then_inc(stats, 1)
                d.wait_ge(stats, k + 7 + ONE)
                nc.vector.scalar_tensor_tensor(out=bias[:], in0=mv[:, :, 0], scalar=-1.0, in1=scale[:], op0=ALU.mult,
                                               op1=ALU.mult).then_inc(stats, 1)

            @block.tensor
            def _(t):
                k = 1 + IMAGES * NBN + IMAGES
                t.wait_ge(loaded, 16 * 5 + ONE)
                t.wait_ge(stats, k + 2 + ONE)
                nc.tensor.matmul(pg[:], avg[:], mv[:].rearrange("p b s -> p (b s)"), start=True, stop=True).then_inc(stats, 1)

            @block.scalar
            def _(a):
                k = 1 + IMAGES * NBN + IMAGES
                a.wait_ge(stats, k + 6 + ONE)
                nc.scalar.activation(sq[:], var[:], ACT.Sqrt, bias=eps5[:]).then_inc(dev, 1)
    return x, scale, bias, loaded, stats


def project(nc, l, x_d, w, xs_d, z_d, normed):
    with Phase(nc, f"proj{l}") as ph:
        N = SUB
        ROWS = N // SIDE
        STEPS = L // N
        if normed:
            x = ph.sb("x", [CH, IMAGES, L])
            loaded = ph.sem("x_loaded")
        else:
            x, scale, bias, _, _ = group_norm_head(nc, ph, x_d, w)
        win = ph.sb("win", [CH, 2, 3, P])
        xn = ph.sb("xn", [CH, 2, IMAGES, N])
        xs_o = ph.sb("xs_o", [P, 2, TILES, ROWS, PADDED])
        z_o = ph.sb("z_o", [P, 2, TILES, N])
        p_xs = ph.ps("p_xs", [P, TILES, 512])
        p_z = ph.ps("p_z", [P, TILES, 512])
        weights = ph.sem("weights")
        zeroed = ph.sem("zeroed")
        xn_ready = ph.sem("xn_ready")
        xs_psum = ph.sem("xs_psum")
        z_psum = ph.sem("z_psum")
        xs_ready = ph.sem("xs_ready")
        z_ready = ph.sem("z_ready")
        xs_stored = [ph.sem(f"xs_stored{j}") for j in range(2)]
        z_stored = [ph.sem(f"z_stored{j}") for j in range(2)]
        with ph.block() as block:
            @block.sync
            def _(sp):
                sp.dma_start(win[:], w["win"]).then_inc(weights, 16)
                if normed:
                    for b in range(IMAGES):
                        sp.dma_start(x[:, b, :], x_d[b]).then_inc(loaded, 16)
                with sp.Fori(0, STEPS // 2) as i:
                    for j in range(2):
                        sp.wait_ge(xs_ready, i * 2 + (j + 1) + ONE)
                        sp.dma_start(xs_d[:, :, bass.ds(i * (2 * ROWS * PADDED) + j * ROWS * PADDED, ROWS * PADDED)],
                                     xs_o[:, j].rearrange("p t r c -> p t (r c)")).then_inc(xs_stored[j], 16)
                        sp.wait_ge(z_ready, i * 2 + (j + 1) + ONE)
                        sp.dma_start(z_d[:, :, bass.ds(i * (2 * N) + j * N, N)], z_o[:, j]).then_inc(z_stored[j], 16)
                for j in range(2):
                    sp.wait_ge(xs_stored[j], 16 * (STEPS // 2) + ONE)
                    sp.wait_ge(z_stored[j], 16 * (STEPS // 2) + ONE)

            @block.gpsimd
            def _(g):
                g.memset(xs_o[:], 0.0).then_inc(zeroed, 1)

            @block.scalar
            def _(a):
                if normed:
                    a.wait_ge(loaded, 32 + ONE)
                with a.Fori(0, STEPS // 2) as i:
                    for j in range(2):
                        a.wait_ge(z_psum, i * 2 + j + ONE)
                        for b in range(IMAGES):
                            src = x[:, b, bass.ds(i * (2 * N) + j * N, N)]
                            if normed:
                                last = nc.scalar.activation(xn[:, j, b, :], src, ACT.Copy)
                            else:
                                last = nc.scalar.activation(xn[:, j, b, :], src, ACT.Identity, bias=bias[:, b:b + 1],
                                                            scale=scale[:, b:b + 1])
                            last.then_inc(xn_ready, 1)
                        a.wait_ge(z_psum, i * 2 + (j + 1) + ONE)
                        a.wait_ge(z_stored[j], i * 16 + ONE)
                        nc.scalar.activation(z_o[:, j], p_z[:, :, 0:N], ACT.Silu).then_inc(z_ready, 1)

            @block.tensor
            def _(t):
                t.wait_ge(weights, 16 + ONE)
                with t.Fori(0, STEPS // 2) as i:
                    for j in range(2):
                        t.wait_ge(xn_ready, i * 4 + (2 * j + 2) + ONE)
                        for half, psum, free, done in ((0, p_xs, xs_ready, xs_psum), (1, p_z, z_ready, z_psum)):
                            t.wait_ge(free, i * 2 + j + ONE)
                            nc.tensor.matmul(psum[:, 0, 0:N], win[:, half, 0, :], xn[:, j, 0, :], start=True, stop=True)
                            nc.tensor.matmul(psum[:, 1, 0:N], win[:, half, 0, :], xn[:, j, 1, :], start=True, stop=True)
                            nc.tensor.matmul(psum[:, 2, 0:N], win[:, half, 1, :], xn[:, j, 0, :], start=True, stop=False)
                            nc.tensor.matmul(psum[:, 2, 0:N], win[:, half, 2, :], xn[:, j, 1, :], start=False,
                                             stop=True).then_inc(done, 1)

            @block.vector
            def _(d):
                d.wait_ge(zeroed, 1 + ONE)
                with d.Fori(0, STEPS // 2) as i:
                    for j in range(2):
                        d.wait_ge(xs_psum, i * 2 + (j + 1) + ONE)
                        d.wait_ge(xs_stored[j], i * 16 + ONE)
                        nc.vector.tensor_copy(xs_o[:, j, :, :, 1:1 + SIDE],
                                              p_xs[:, :, 0:N].rearrange("p t (r c) -> p t r c", c=SIDE)).then_inc(xs_ready, 1)


def conv_depthwise(nc, l, w, xs_d, u_d):
    with Phase(nc, f"conv{l}") as ph:
        N = SUB
        ROWS = N // SIDE
        STEPS = L // N
        grid = ph.sb("grid", [P, TILES, PADDED, PADDED])
        taps = ph.sb("taps", [P, TAPS, 2, P])
        bias = ph.sb("bias", [P, TILES])
        u_o = ph.sb("u_o", [P, 2, TILES, N])
        psum = [ph.ps(f"psum{j}", [P, TILES, 512]) for j in range(2)]
        loaded = ph.sem("loaded")
        edges = ph.sem("edges")
        conv_done = ph.sem("conv_done")
        u_ready = ph.sem("u_ready")
        u_stored = [ph.sem(f"u_stored{j}") for j in range(2)]
        with ph.block() as block:
            @block.sync
            def _(sp):
                sp.dma_start(taps[:], w["taps"]).then_inc(loaded, 16)
                sp.dma_start(bias[:], w["conv_b"]).then_inc(loaded, 16)
                for t in range(TILES):
                    sp.dma_start(grid[:, t, 1:1 + SIDE, :].rearrange("p r c -> p (r c)"), xs_d[:, t, :]).then_inc(loaded, 16)
                with sp.Fori(0, STEPS // 2) as i:
                    for j in range(2):
                        sp.wait_ge(u_ready, i * 2 + (j + 1) + ONE)
                        sp.dma_start(u_d[:, :, bass.ds(i * (2 * N) + j * N, N)], u_o[:, j]).then_inc(u_stored[j], 16)
                for j in range(2):
                    sp.wait_ge(u_stored[j], 16 * (STEPS // 2) + ONE)

            @block.gpsimd
            def _(g):
                g.memset(grid[:, :, 0, :], 0.0).then_inc(edges, 1)
                g.memset(grid[:, :, PADDED - 1, :], 0.0).then_inc(edges, 1)

            @block.tensor
            def _(t):
                t.wait_ge(loaded, 16 * (2 + TILES) + ONE)
                t.wait_ge(edges, 2 + ONE)
                with t.Fori(0, STEPS // 2) as i:
                    for j in range(2):
                        t.wait_ge(u_stored[j], i * 16 + ONE)
                        for m in range(TILES):
                            for tap in range(TAPS):
                                dy, dx = divmod(tap, 3)
                                last = nc.tensor.matmul(psum[j][:, m, 0:N], taps[:, tap, m // 2, :],
                                                        grid[:, m, bass.ds(i * (2 * ROWS) + (j * ROWS + dy), ROWS), dx:dx + SIDE],
                                                        start=(tap == 0), stop=(tap == TAPS - 1))
                        last.then_inc(conv_done, 1)

            @block.scalar
            def _(a):
                a.wait_ge(loaded, 16 * (2 + TILES) + ONE)
                with a.Fori(0, STEPS // 2) as i:
                    for j in range(2):
                        a.wait_ge(conv_done, i * 2 + (j + 1) + ONE)
                        for m in range(TILES):
                            last = nc.scalar.activation(u_o[:, j, m, :], psum[j][:, m, 0:N], ACT.Silu, bias=bias[:, m:m + 1])
                        last.then_inc(u_ready, 1)


def conv_sampled(nc, w, xs_d, u_d):
    with Phase(nc, "conv0") as ph:
        N = SUB
        ROWS = N // SIDE
        STEPS = L // N
        grid = ph.sb("grid", [P, TILES, PADDED, PADDED])
        taps = ph.sb("taps", [P, TAPS, 6, P])
        bn = ph.sb("bn", [P, 5, TILES])
        scale = ph.sb("scale", [P, TILES])
        shift = ph.sb("shift", [P, TILES])
        tmp = ph.sb("tmp", [P, TILES])
        eps = ph.sb("eps", [P, 1])
        off_w = ph.sb("off_w", [P, TILES, 4])
        off_sel = ph.sb("off_sel", [4, 2, TILES, P])
        gel = ph.sb("gel", [P, TILES, N])
        frac = ph.sb("frac", [4, 2, N])
        diff = ph.sb("diff", [P, ROWS + 1, SIDE])
        top = ph.sb("top", [P, ROWS, SIDE])
        bot = ph.sb("bot", [P, ROWS, SIDE])
        u_o = ph.sb("u_o", [P, 2, TILES, N])
        p_conv = ph.ps("p_conv", [P, TILES, 512])
        p_off = ph.ps("p_off", [4, 512])
        p_frac = [ph.ps(f"p_frac{j}", [P, 2, 512]) for j in range(2)]
        loaded = ph.sem("loaded")
        edges = ph.sem("edges")
        consts = ph.sem("consts")
        conv_done = ph.sem("conv_done")
        gelu_done = ph.sem("gelu_done")
        off_done = ph.sem("off_done")
        tanh_done = ph.sem("tanh_done")
        frac_ready = ph.sem("frac_ready")
        spread = ph.sem("spread")
        lerp = ph.sem("lerp")
        u_stored = [ph.sem(f"u_stored{j}") for j in range(2)]
        passed = ph.sem("passed")
        STEP = 8
        FEEDS = [[(0, 0), (2, 1)], [(1, 0), (2, 2)], [(0, 3), (1, 4), (2, 5)]]
        with ph.block() as block:
            @block.sync
            def _(sp):
                for dst, src in ((taps, w["taps"]), (bn, w["bn"]), (off_w, w["off_w"]), (off_sel, w["off_sel"])):
                    sp.dma_start(dst[:], src).then_inc(loaded, 16)
                for t in range(TILES):
                    sp.dma_start(grid[:, t, 1:1 + SIDE, :].rearrange("p r c -> p (r c)"), xs_d[:, t, :]).then_inc(loaded, 16)
                with sp.Fori(0, STEPS // 2) as i:
                    for j in range(2):
                        sp.wait_ge(lerp, i * (2 * 3 * STEP) + (j + 1) * 3 * STEP + ONE)
                        sp.dma_start(u_d[:, :, bass.ds(i * (2 * N) + j * N, N)], u_o[:, j]).then_inc(u_stored[j], 16)
                for j in range(2):
                    sp.wait_ge(u_stored[j], 16 * (STEPS // 2) + ONE)

            @block.gpsimd
            def _(g):
                g.memset(grid[:, :, 0, :], 0.0).then_inc(edges, 1)
                g.memset(grid[:, :, PADDED - 1, :], 0.0).then_inc(edges, 1)
                with g.Fori(0, STEPS // 2) as i:
                    for j in range(2):
                        g.wait_ge(tanh_done, i * 2 + (j + 1) + ONE)
                        g.wait_ge(spread, i * 6 + 3 * j + ONE)
                        g.sem_inc(passed, 1)
                        g.tensor_scalar(frac[:, 1, :], frac[:, 0, :], 0.5, 0.5, ALU.mult, ALU.add).then_inc(frac_ready, 1)

            @block.tensor
            def _(t):
                t.wait_ge(loaded, 16 * 7 + ONE)
                t.wait_ge(edges, 2 + ONE)
                with t.Fori(0, STEPS // 2) as i:
                    for j in range(2):
                        t.wait_ge(gelu_done, i * 6 + 3 * j + ONE)
                        for m in range(TILES):
                            n = 0
                            for tap in range(TAPS):
                                dy, dx = divmod(tap, 3)
                                for src, blk in FEEDS[m]:
                                    last = nc.tensor.matmul(p_conv[:, m, 0:N], taps[:, tap, blk, :],
                                                            grid[:, src, bass.ds(i * (2 * ROWS) + (j * ROWS + dy), ROWS), dx:dx + SIDE],
                                                            start=(n == 0), stop=(n == TAPS * len(FEEDS[m]) - 1))
                                    n += 1
                        last.then_inc(conv_done, 1)
                        t.wait_ge(gelu_done, i * 6 + (3 * j + 3) + ONE)
                        for m in range(TILES):
                            last = nc.tensor.matmul(p_off[:, 0:N], off_w[:, m, :], gel[:, m, :], start=(m == 0), stop=(m == 2))
                        last.then_inc(off_done, 1)
                        t.wait_ge(frac_ready, i * 2 + (j + 1) + ONE)
                        for m in range(TILES):
                            v = 3 * j + m
                            t.wait_ge(lerp, i * (6 * STEP) + max(v - 1, 0) * STEP + ONE)
                            for axis in range(2):
                                last = nc.tensor.matmul(p_frac[v % 2][:, axis, 0:N], off_sel[:, axis, m, :], frac[:, 1, :],
                                                        start=True, stop=True)
                            last.then_inc(spread, 1)

            @block.scalar
            def _(a):
                a.wait_ge(loaded, 16 * 7 + ONE)
                a.wait_ge(consts, 1 + ONE)
                nc.scalar.activation(tmp[:], bn[:, 4, :], ACT.Sqrt, bias=eps[:]).then_inc(consts, 1)
                a.wait_ge(consts, 7 + ONE)
                with a.Fori(0, STEPS // 2) as i:
                    for j in range(2):
                        a.wait_ge(conv_done, i * 2 + (j + 1) + ONE)
                        a.wait_ge(off_done, i * 2 + j + ONE)
                        for m in range(TILES):
                            nc.scalar.activation(gel[:, m, :], p_conv[:, m, 0:N], ACT.Gelu, bias=shift[:, m:m + 1],
                                                 scale=scale[:, m:m + 1]).then_inc(gelu_done, 1)
                        a.wait_ge(off_done, i * 2 + (j + 1) + ONE)
                        a.wait_ge(frac_ready, i * 2 + j + ONE)
                        nc.scalar.activation(frac[:, 0, :], p_off[:, 0:N], ACT.Tanh).then_inc(tanh_done, 1)

            @block.vector
            def _(d):
                nc.vector.memset(eps[:], 1e-5).then_inc(consts, 1)
                d.wait_ge(consts, 2 + ONE)
                nc.vector.reciprocal(scale[:], tmp[:]).then_inc(consts, 1)
                d.wait_ge(consts, 3 + ONE)
                nc.vector.tensor_tensor(scale[:], scale[:], bn[:, 1, :], ALU.mult).then_inc(consts, 1)
                nc.vector.tensor_tensor(shift[:], bn[:, 0, :], bn[:, 3, :], ALU.subtract).then_inc(consts, 1)
                d.wait_ge(consts, 5 + ONE)
                nc.vector.tensor_tensor(tmp[:], shift[:], scale[:], ALU.mult).then_inc(consts, 1)
                d.wait_ge(consts, 6 + ONE)
                nc.vector.tensor_tensor(shift[:], tmp[:], bn[:, 2, :], ALU.add).then_inc(consts, 1)
                d.wait_ge(loaded, 16 * 7 + ONE)
                d.wait_ge(edges, 2 + ONE)
                with d.Fori(0, STEPS // 2) as i:
                    for j in range(2):
                        for m in range(TILES):
                            v = 3 * j + m
                            s = i * (6 * STEP) + v * STEP
                            r0 = i * (2 * ROWS) + (j * ROWS + 1)
                            fy = p_frac[v % 2][:, 0, 0:N].rearrange("p (r c) -> p r c", c=SIDE)
                            fx = p_frac[v % 2][:, 1, 0:N].rearrange("p (r c) -> p r c", c=SIDE)
                            here = grid[:, m, bass.ds(r0, ROWS), 1:1 + SIDE]
                            below = grid[:, m, bass.ds(r0 + 1, ROWS), 1:1 + SIDE]
                            d.wait_ge(lerp, s + ONE)
                            nc.vector.tensor_tensor(diff[:], grid[:, m, bass.ds(r0, ROWS + 1), 2:2 + SIDE],
                                                    grid[:, m, bass.ds(r0, ROWS + 1), 1:1 + SIDE], ALU.subtract).then_inc(lerp, 1)
                            d.wait_ge(spread, i * 6 + (v + 1) + ONE)
                            d.wait_ge(lerp, s + 1 + ONE)
                            nc.vector.tensor_tensor(top[:], diff[:, 0:ROWS, :], fx, ALU.mult).then_inc(lerp, 1)
                            nc.vector.tensor_tensor(bot[:], diff[:, 1:ROWS + 1, :], fx, ALU.mult).then_inc(lerp, 1)
                            d.wait_ge(lerp, s + 2 + ONE)
                            nc.vector.tensor_tensor(top[:], top[:], here, ALU.add).then_inc(lerp, 1)
                            d.wait_ge(lerp, s + 3 + ONE)
                            nc.vector.tensor_tensor(bot[:], bot[:], below, ALU.add).then_inc(lerp, 1)
                            d.wait_ge(lerp, s + 5 + ONE)
                            nc.vector.tensor_tensor(bot[:], bot[:], top[:], ALU.subtract).then_inc(lerp, 1)
                            d.wait_ge(lerp, s + 6 + ONE)
                            nc.vector.tensor_tensor(bot[:], bot[:], fy, ALU.mult).then_inc(lerp, 1)
                            d.wait_ge(lerp, s + 7 + ONE)
                            d.wait_ge(u_stored[j], i * 16 + ONE)
                            nc.vector.tensor_tensor(u_o[:, j, m, :].rearrange("p (r c) -> p r c", c=SIDE), bot[:], top[:],
                                                    ALU.add).then_inc(lerp, 1)


def prepare(nc, l, w, map_d, map_cols, delta_d, du_d, bc_d, useq_d):
    with Phase(nc, f"prep{l}") as ph:
        causal = l == 1
        DW = CHUNK
        grid = ph.sb("grid", [P, TILES, SIDE * map_cols])
        useq = ph.sb("useq", [P, 2, TILES, DW])
        HALO = SEQ_TAPS - 1
        if causal:
            raw = ph.sb("raw", [P, TILES, HALO + DW])
            halo = ph.sb("halo", [P, TILES, HALO])
            taps = ph.sb("taps", [P, SEQ_TAPS, 2, P])
            conv_b = ph.sb("conv_b", [P, TILES])
            p_conv = ph.ps("p_conv", [P, 2, 512])
        wx = ph.sb("wx", [P, DIRS, TILES, DBL_ROWS])
        wdt = ph.sb("wdt", [BC_ROWS + IMAGES * RANK, DIRS, TILES, P])
        dtb = ph.sb("dtb", [P, DIRS, TILES])
        dtv = ph.sb("dtv", [DBL_ROWS, DW])
        hi = ph.sb("hi", [BC_ROWS, DW], BF16)
        mid = ph.sb("mid", [BC_ROWS, DW], BF16)
        lo = ph.sb("lo", [BC_ROWS, DW], BF16)
        rest = ph.sb("rest", [BC_ROWS, DW])
        sp_b = ph.sb("softplus", [P, 2, DW])
        delta = ph.sb("delta", [P, 2, DW])
        du = ph.sb("du", [P, 2, DW])
        p_dbl = ph.ps("p_dbl", [DBL_ROWS, 3, 512])
        p_dt = ph.ps("p_dt", [P, 3, 512])
        passed = ph.sem("passed")
        sp_passed = ph.sem("sp_passed")
        loaded = ph.sem("loaded")
        raw_ready = ph.sem("raw_ready")
        halo_ready = ph.sem("halo_ready")
        conv_done = ph.sem("conv_done")
        useq_ready = ph.sem("useq_ready")
        useq_stored = [ph.sem(f"useq_stored{j}") for j in range(2)]
        dbl_done = ph.sem("dbl_done")
        dtv_ready = ph.sem("dtv_ready")
        hi_ready = ph.sem("hi_ready")
        rest_ready = ph.sem("rest_ready")
        mid_ready = ph.sem("mid_ready")
        lo_ready = ph.sem("lo_ready")
        bc_stored = ph.sem("bc_stored")
        dt_done = ph.sem("dt_done")
        capped = ph.sem("capped")
        exp_done = ph.sem("exp_done")
        log_done = ph.sem("log_done")
        delta_ready = ph.sem("delta_ready")
        du_ready = ph.sem("du_ready")
        reset_done = ph.sem("reset_done")
        delta_stored = [ph.sem(f"delta_stored{j}") for j in range(2)]
        du_stored = [ph.sem(f"du_stored{j}") for j in range(2)]
        walks = WALKS[l]
        n_loads = 3 + TILES + (2 if causal else 0)
        PAIRS = 2 if walks[0][0] == "window" or walks[0][2] == "snake" else 1
        grids = [grid[:, m, :].rearrange("p (r c) -> p r c", c=map_cols)[:, :, (map_cols - SIDE) // 2:(map_cols - SIDE) // 2 + SIDE]
                 for m in range(TILES)]
        flat = useq_d is not None
        DU_FREE = TILES

        with ph.block() as block:
            @block.sync
            def _(sp):
                for dst, src in ((wx, w["wx"]), (dtb, w["dtb"])):
                    sp.dma_start(dst[:], src).then_inc(loaded, 16)
                sp.dma_start(wdt[BC_ROWS:DBL_ROWS], w["wdt"]).then_inc(loaded, 16)
                if causal:
                    sp.dma_start(taps[:], w["taps"]).then_inc(loaded, 16)
                    sp.dma_start(conv_b[:], w["conv_b"]).then_inc(loaded, 16)
                for m in range(TILES):
                    sp.dma_start(grid[:, m, :], map_d[:, m, :]).then_inc(loaded, 16)
                with sp.Fori(0, DIRS * CHUNKS // 2) as i:
                    for j in range(2):
                        at = i * (2 * DW) + j * DW
                        if flat:
                            sp.wait_ge(useq_ready, i * 18 + (9 * j + 9) + ONE)
                            sp.dma_start(useq_d[:, :, bass.ds(at, DW)], useq[:, j]).then_inc(useq_stored[j], 16)
                        for part, (buf, ready) in enumerate(((hi, hi_ready), (mid, mid_ready), (lo, lo_ready))):
                            sp.wait_ge(ready, i * 2 + (j + 1) + ONE)
                            sp.sem_inc(sp_passed, 1)
                            rows = IMAGES * STATES
                            for t in range(2):
                                sp.dma_start(bc_d[t, part * rows:(part + 1) * rows, bass.ds(at, DW)],
                                             buf[t * rows:(t + 1) * rows, :]).then_inc(bc_stored, 16)
                        for m in range(TILES):
                            v = 3 * j + m
                            sp.wait_ge(du_ready, i * 6 + (DU_FREE + v + 1) + ONE)
                            sp.sem_inc(sp_passed, 1)
                            sp.dma_start(du_d[:, m, bass.ds(at, DW)], du[:, v % 2, :]).then_inc(du_stored[v % 2], 16)
                            if l == 0:
                                sp.wait_ge(reset_done, i * 6 + (v + 1) + ONE)
                            sp.dma_start(delta_d[:, m, bass.ds(at, DW)], delta[:, v % 2, :]).then_inc(delta_stored[v % 2], 16)
                sp.wait_ge(bc_stored, 16 * 6 * DIRS * CHUNKS + ONE)
                for j in range(2):
                    sp.wait_ge(delta_stored[j], 16 * TILES * DIRS * CHUNKS // 2 + ONE)
                    sp.wait_ge(du_stored[j], 16 * TILES * DIRS * CHUNKS // 2 + ONE)
                    if flat:
                        sp.wait_ge(useq_stored[j], 16 * DIRS * CHUNKS // 2 + ONE)

            @block.gpsimd
            def _(g):
                g.wait_ge(loaded, 16 * n_loads + ONE)
                for k in range(DIRS):
                    if causal:
                        g.wait_ge(halo_ready, k * 2 * CHUNKS + k + ONE)
                        g.memset(halo[:], 0.0).then_inc(halo_ready, 1)
                    with g.Fori(0, CHUNKS // 2) as i:
                        for j in range(2):
                            c = i * 2 + j
                            it = i * 2 + (k * CHUNKS + j)
                            if causal:
                                g.wait_ge(conv_done, it * 9 + ONE)
                                g.wait_ge(halo_ready, it * 2 + (k + 1) + ONE)
                                g.sem_inc(passed, 1)
                                g.tensor_copy(raw[:, :, 0:HALO], halo[:]).then_inc(halo_ready, 1)
                                for m in range(TILES):
                                    for src, dst in walk_pairs(walks[k], c, grids[m], raw[:, m, HALO:HALO + DW]):
                                        g.tensor_copy(dst, src).then_inc(raw_ready, 1)
                                g.wait_ge(raw_ready, it * TILES + TILES + ONE)
                                g.wait_ge(halo_ready, it * 2 + (k + 2) + ONE)
                                g.sem_inc(passed, 1)
                                g.tensor_copy(halo[:], raw[:, :, DW:DW + HALO]).then_inc(halo_ready, 1)
                            else:
                                g.wait_ge(du_ready, it * 3 + ONE)
                                for m in range(TILES):
                                    for src, dst in walk_pairs(walks[k], c, grids[m], useq[:, j, m, :]):
                                        g.tensor_copy(dst, src).then_inc(useq_ready, 1)

            @block.tensor
            def _(t):
                t.wait_ge(loaded, 16 * n_loads + ONE)
                for k in range(DIRS):
                    with t.Fori(0, CHUNKS // 2) as i:
                        for j in range(2):
                            it = i * 2 + (k * CHUNKS + j)
                            if causal:
                                t.wait_ge(raw_ready, it * TILES + TILES + ONE)
                                t.wait_ge(halo_ready, it * 2 + (k + 2) + ONE)
                                for m in range(TILES):
                                    for n in range(3):
                                        q = m * 3 + n
                                        t.wait_ge(useq_ready, it * 9 + max(q - 1, 0) + ONE)
                                        for tap in range(SEQ_TAPS):
                                            last = nc.tensor.matmul(p_conv[:, (q + j) % 2, 0:SUB], taps[:, tap, m // 2, :],
                                                                    raw[:, m, n * SUB + tap:n * SUB + tap + SUB],
                                                                    start=(tap == 0), stop=(tap == SEQ_TAPS - 1))
                                        last.then_inc(conv_done, 1)
                                t.wait_ge(useq_ready, it * 9 + 9 + ONE)
                            else:
                                t.wait_ge(useq_ready, it * (TILES * PAIRS) + TILES * PAIRS + ONE)
                            t.wait_ge(rest_ready, it + ONE)
                            t.wait_ge(dtv_ready, it + ONE)
                            for n in range(3):
                                for m in range(TILES):
                                    last = nc.tensor.matmul(p_dbl[:, n, 0:SUB], wx[:, k, m, :], useq[:, j, m, n * SUB:(n + 1) * SUB],
                                                            start=(m == 0), stop=(m == 2))
                            last.then_inc(dbl_done, 1)
                            t.wait_ge(dtv_ready, it + 1 + ONE)
                            for m in range(TILES):
                                t.wait_ge(delta_ready, it * 3 + m + ONE)
                                for n in range(3):
                                    last = nc.tensor.matmul(p_dt[:, n, 0:SUB], wdt[BC_ROWS:DBL_ROWS, k, m, :],
                                                            dtv[BC_ROWS:DBL_ROWS, n * SUB:(n + 1) * SUB], start=True, stop=True)
                                last.then_inc(dt_done, 1)

            @block.scalar
            def _(a):
                a.wait_ge(loaded, 16 * n_loads + ONE)
                for k in range(DIRS):
                    with a.Fori(0, CHUNKS // 2) as i:
                        for j in range(2):
                            it = i * 2 + (k * CHUNKS + j)
                            if causal:
                                a.wait_ge(du_ready, it * 3 + ONE)
                                a.wait_ge(useq_stored[j], i * 16 + k * (16 * CHUNKS // 2) + ONE)
                                for q in range(9):
                                    a.wait_ge(conv_done, it * 9 + (q + 1) + ONE)
                                    nc.scalar.activation(useq[:, j, q // 3, (q % 3) * SUB:(q % 3 + 1) * SUB],
                                                         p_conv[:, (q + j) % 2, 0:SUB], ACT.Silu,
                                                         bias=conv_b[:, q // 3:q // 3 + 1]).then_inc(useq_ready, 1)
                            a.wait_ge(dbl_done, it + 1 + ONE)
                            a.wait_ge(dt_done, it * 3 + ONE)
                            nc.scalar.activation(dtv[BC_ROWS:DBL_ROWS, :].rearrange("p (n s) -> p n s", n=3),
                                                 p_dbl[BC_ROWS:DBL_ROWS, :, 0:SUB], ACT.Copy).then_inc(dtv_ready, 1)
                            a.wait_ge(bc_stored, it * 96 + ONE)
                            a.wait_ge(lo_ready, it + ONE)
                            nc.scalar.activation(hi[:].rearrange("p (n s) -> p n s", n=3), p_dbl[0:BC_ROWS, :, 0:SUB],
                                                 ACT.Copy).then_inc(hi_ready, 1)
                            a.wait_ge(rest_ready, it + 1 + ONE)
                            nc.scalar.activation(mid[:], rest[:], ACT.Copy).then_inc(mid_ready, 1)
                            for m in range(TILES):
                                v = 3 * j + m
                                a.wait_ge(capped, it * 3 + (m + 1) + ONE)
                                nc.scalar.activation(sp_b[:, v % 2, :], sp_b[:, v % 2, :], ACT.Exp).then_inc(exp_done, 1)
                                a.wait_ge(exp_done, it * 3 + (m + 1) + ONE)
                                nc.scalar.activation(sp_b[:, v % 2, :], sp_b[:, v % 2, :], ACT.Ln, bias=1.0).then_inc(log_done, 1)

            @block.vector
            def _(d):
                d.sem_inc(du_ready, DU_FREE)
                d.wait_ge(loaded, 16 * n_loads + ONE)
                for k in range(DIRS):
                    with d.Fori(0, CHUNKS // 2) as i:
                        for j in range(2):
                            it = i * 2 + (k * CHUNKS + j)
                            d.wait_ge(hi_ready, it + 1 + ONE)
                            d.wait_ge(lo_ready, it + ONE)
                            nc.vector.tensor_tensor(rest[:].rearrange("p (n s) -> p n s", n=3), p_dbl[0:BC_ROWS, :, 0:SUB],
                                                    hi[:].rearrange("p (n s) -> p n s", n=3), ALU.subtract).then_inc(rest_ready, 1)
                            d.wait_ge(mid_ready, it + 1 + ONE)
                            nc.vector.tensor_tensor(lo[:], rest[:], mid[:], ALU.subtract).then_inc(lo_ready, 1)
                            for m in range(TILES):
                                v = 3 * j + m
                                x3 = p_dt[:, :, 0:SUB]
                                b = dtb[:, k, m:m + 1]
                                d.wait_ge(dt_done, it * 3 + (m + 1) + ONE)
                                d.wait_ge(delta_ready, it * 3 + m + ONE)
                                nc.vector.tensor_scalar(sp_b[:, v % 2, :].rearrange("p (n s) -> p n s", n=3), x3, b, 40.0,
                                                        ALU.add, ALU.min).then_inc(capped, 1)
                                d.wait_ge(log_done, it * 3 + (m + 1) + ONE)
                                uses = i * 48 + (k * (CHUNKS // 2) * 48 + 16 * (v // 2))
                                d.wait_ge(delta_stored[v % 2], uses + ONE)
                                d.wait_ge(du_stored[v % 2], uses + ONE)
                                nc.vector.scalar_tensor_tensor(out=delta[:, v % 2, :].rearrange("p (n s) -> p n s", n=3), in0=x3,
                                                               scalar=b, in1=sp_b[:, v % 2, :].rearrange("p (n s) -> p n s", n=3),
                                                               op0=ALU.add, op1=ALU.max).then_inc(delta_ready, 1)
                                d.wait_ge(delta_ready, it * 3 + (m + 1) + ONE)
                                nc.vector.tensor_tensor(du[:, v % 2, :], delta[:, v % 2, :], useq[:, j, m, :],
                                                        ALU.mult).then_inc(du_ready, 1)
                                if l == 0:
                                    d.wait_ge(du_ready, it * 3 + (DU_FREE + m + 1) + ONE)
                                    nc.vector.memset(delta[:, v % 2, :].rearrange("p (w n) -> p w n", n=WINDOW)[:, :, 0:1],
                                                     RESET_DELTA).then_inc(reset_done, 1)


STEP_T = 1024
SCAN_CHUNKS = L // STEP_T
UNROLL = 3
UNITS = TILES * STATES
DA_SLOTS = 3
DBU_SLOTS = 3
H_SLOTS = 6
HC_SLOTS = 6
C_SLOTS = 2
BANK_SLOTS = 3
REDUCE_LAG = 5
EVAC_AT = 5
ROUND = UNROLL * UNITS


def on_pool(u):
    return u % 3 != 2


def pool_units(u):
    return (u // 3) * 2 + min(u % 3, 2)


def scan(nc, l, w, delta_d, du_d, bc_d, y_d):
    with Phase(nc, f"scan{l}") as ph:
        T = STEP_T
        H = T // 2
        a_all = ph.sb("a_all", [P, DIRS, UNITS])
        a_cur = ph.sb("a_cur", [P, UNITS])
        sel = ph.sb("sel", [PARTS * IMAGES * STATES, UNITS, P], BF16)
        eye = ph.sb("eye", [P, P])
        delta = ph.sb("delta", [P, UNROLL, TILES, T])
        du = ph.sb("du", [P, UNROLL, TILES, T])
        bc = ph.sb("bc", [PARTS * IMAGES * STATES, UNROLL, 2, T], BF16)
        da = ph.sb("da", [P, DA_SLOTS, T])
        dbu = ph.sb("dbu", [P, DBU_SLOTS, T])
        h = ph.sb("h", [P, H_SLOTS, T])
        hc = ph.sb("hc", [P, HC_SLOTS, T])
        c_sb = ph.sb("c_sb", [P, C_SLOTS, T])
        y = ph.sb("y", [P, TILES, T])
        state = ph.sb("state", [P, UNITS])
        spread = [ph.ps(f"spread{s}", [P, T]) for s in range(BANK_SLOTS)]
        p_y = ph.ps("p_y", [P, T])
        consts = ph.sem("consts")
        a_ready = ph.sem("a_ready")
        loaded = [ph.sem(f"loaded{s}") for s in range(UNROLL)]
        da_ready = ph.sem("da_ready")
        b_spread = ph.sem("b_spread")
        c_spread_pool = ph.sem("c_spread_pool")
        c_spread_vec = ph.sem("c_spread_vec")
        c_copied = ph.sem("c_copied")
        dbu_ready = ph.sem("dbu_ready")
        scanned = ph.sem("scanned")
        hc_vector = ph.sem("hc_vector")
        hc_pool = ph.sem("hc_pool")
        state_ready = ph.sem("state_ready")
        passed = ph.sem("passed")
        reduced = ph.sem("reduced")
        y_ready = ph.sem("y_ready")
        y_stored = ph.sem("y_stored")
        LOADS = 3 * 16
        ROUNDS = SCAN_CHUNKS // UNROLL
        ALL = DIRS * SCAN_CHUNKS
        R_POOL = pool_units(ROUND)
        R_VEC = ROUND - R_POOL

        order = []
        for s in range(ROUND + 2):
            if s < ROUND:
                order.append(("b", s))
            if 1 <= s <= ROUND and on_pool(s - 1):
                order.append(("c", s - 1))
            if s >= 2 and not on_pool(s - 2):
                order.append(("c", s - 2))
        place = {item: n for n, item in enumerate(order)}
        assert len(order) % BANK_SLOTS == 0

        def bank(kind, u):
            return spread[place[(kind, u)] % BANK_SLOTS][:]

        def wait_product(eng, u, round_pool, round_vec):
            if on_pool(u):
                eng.wait_ge(hc_pool, round_pool + (pool_units(u) + 1) + ONE)
            else:
                eng.wait_ge(hc_vector, round_vec + (u - pool_units(u) + 1) + ONE)

        with ph.block() as block:
            @block.sync
            def _(sp):
                sp.dma_start(a_all[:], w["alog"]).then_inc(consts, 16)
                sp.dma_start(sel[:].bitcast(U16), w["sel"]).then_inc(consts, 16)
                sp.dma_start(eye[:], w["eye"]).then_inc(consts, 16)

                def load(at, s):
                    sp.dma_start(delta[:, s], delta_d[:, :, bass.ds(at, T)]).then_inc(loaded[s], 16)
                    sp.dma_start(du[:, s], du_d[:, :, bass.ds(at, T)]).then_inc(loaded[s], 16)
                    sp.dma_start(bc[:, s], bc_d[:, :, bass.ds(at, T)].rearrange("t r n -> r t n")).then_inc(loaded[s], 16)

                def store(g, at):
                    sp.wait_ge(y_ready, g * TILES + TILES + ONE)
                    sp.dma_start(y_d[:, :, bass.ds(at, T)], y[:]).then_inc(y_stored, 16)

                for s in range(UNROLL):
                    load(s * T, s)
                with sp.Fori(0, ALL // UNROLL - 1) as i:
                    for s in range(UNROLL):
                        store(i * UNROLL + s, i * (UNROLL * T) + s * T)
                        load(i * (UNROLL * T) + (s + UNROLL) * T, s)
                for s in range(UNROLL):
                    store(ALL - UNROLL + s, (ALL - UNROLL + s) * T)
                sp.wait_ge(y_stored, 16 * ALL + ONE)

            @block.gpsimd
            def _(g):
                with g.Fori(0, DIRS) as k:
                    g.wait_ge(scanned, k * (SCAN_CHUNKS * UNITS) + ONE)
                    g.wait_ge(state_ready, k * ((SCAN_CHUNKS + 1) * UNITS) + ONE)
                    g.sem_inc(passed, 1)
                    g.memset(state[:], 0.0).then_inc(state_ready, UNITS)
                    g.wait_ge(state_ready, k * ((SCAN_CHUNKS + 1) * UNITS) + UNITS + ONE)
                    g.sem_inc(passed, 1)
                    with g.Fori(0, ROUNDS) as r:
                        q = k * (SCAN_CHUNKS * UNITS) + r * ROUND
                        q_pool = k * (ROUNDS * R_POOL) + r * R_POOL
                        for u in range(ROUND):
                            g.wait_ge(scanned, q + (u + 1) + ONE)
                            g.sem_inc(passed, 1)
                            g.tensor_copy(state[:, u % UNITS:u % UNITS + 1], h[:, u % H_SLOTS, T - 1:T]).then_inc(state_ready, 1)
                            if on_pool(u):
                                n = pool_units(u)
                                g.wait_ge(reduced, q + max(u - HC_SLOTS + 1, 0) + ONE)
                                g.wait_ge(c_copied, q_pool + (n + 1) + ONE)
                                nc.gpsimd.tensor_tensor(hc[:, u % HC_SLOTS, :], c_sb[:, n % C_SLOTS, :], h[:, u % H_SLOTS, :],
                                                        ALU.mult).then_inc(hc_pool, 1)

            @block.scalar
            def _(a):
                a.wait_ge(consts, 48 + ONE)
                nc.scalar.activation(a_all[:], a_all[:], ACT.Exp).then_inc(a_ready, 1)
                with a.Fori(0, DIRS) as k:
                    a.wait_ge(a_ready, k + 1 + ONE)
                    a.wait_ge(da_ready, k * (SCAN_CHUNKS * UNITS) + ONE)
                    nc.scalar.activation(a_cur[:], a_all[:, bass.ds(k, 1), :].rearrange("p k u -> p (k u)"), ACT.Copy,
                                         scale=-1.0).then_inc(a_ready, 1)
                    a.wait_ge(a_ready, k + 2 + ONE)
                    with a.Fori(0, ROUNDS) as r:
                        q = k * (SCAN_CHUNKS * UNITS) + r * ROUND
                        q_pool = k * (ROUNDS * R_POOL) + r * R_POOL
                        chunks = k * SCAN_CHUNKS + r * UNROLL

                        def evacuate(t):
                            a.wait_ge(reduced, q + (t + 1) * STATES + ONE)
                            if t % TILES == 0:
                                a.wait_ge(y_stored, chunks * 16 + 16 * (t // TILES) + ONE)
                            nc.scalar.activation(y[:, t % TILES, :], p_y[:], ACT.Copy).then_inc(y_ready, 1)

                        def copy_c(u):
                            n = pool_units(u)
                            a.wait_ge(c_spread_pool, q_pool + (n + 1) + ONE)
                            a.wait_ge(hc_pool, q_pool + max(n - C_SLOTS + 1, 0) + ONE)
                            nc.scalar.activation(c_sb[:, n % C_SLOTS, :], bank("c", u), ACT.Copy).then_inc(c_copied, 1)

                        for u in range(ROUND + 1):
                            if u < ROUND:
                                s, v = divmod(u, UNITS)
                                if v == 0:
                                    a.wait_ge(loaded[s], k * (LOADS * ROUNDS) + r * LOADS + LOADS + ONE)
                                a.wait_ge(scanned, q + max(u - DA_SLOTS + 1, 0) + ONE)
                                nc.scalar.activation(da[:, u % DA_SLOTS, :], delta[:, s, v // STATES, :], ACT.Exp,
                                                     scale=a_cur[:, v:v + 1]).then_inc(da_ready, 1)
                            if u >= 1 and on_pool(u - 1):
                                copy_c(u - 1)
                            if u % STATES == EVAC_AT and u > STATES:
                                evacuate(u // STATES - 1)
                        evacuate(UNROLL * TILES - 1)

            @block.tensor
            def _(t):
                t.wait_ge(consts, 48 + ONE)
                with t.Fori(0, DIRS) as k:
                    with t.Fori(0, ROUNDS) as r:
                        q = k * (SCAN_CHUNKS * UNITS) + r * ROUND
                        q_pool = k * (ROUNDS * R_POOL) + r * R_POOL
                        q_vec = k * (ROUNDS * R_VEC) + r * R_VEC
                        tiles = k * (SCAN_CHUNKS * TILES) + r * (UNROLL * TILES)

                        def make(kind, u):
                            n = place[(kind, u)]
                            if kind == "b" and u % UNITS == 0:
                                t.wait_ge(loaded[u // UNITS], k * (LOADS * ROUNDS) + r * LOADS + LOADS + ONE)
                            if n < BANK_SLOTS:
                                was, v = order[len(order) - BANK_SLOTS + n]
                                assert was == "c" or v < ROUND
                                t.wait_ge(c_copied, q_pool + ONE)
                                t.wait_ge(hc_vector, q_vec + ONE)
                            else:
                                was, v = order[n - BANK_SLOTS]
                                if was == "b":
                                    t.wait_ge(dbu_ready, q + (v + 1) + ONE)
                                elif on_pool(v):
                                    t.wait_ge(c_copied, q_pool + (pool_units(v) + 1) + ONE)
                                else:
                                    t.wait_ge(hc_vector, q_vec + (v - pool_units(v) + 1) + ONE)
                            for half in range(2):
                                last = nc.tensor.matmul(bank(kind, u)[:, half * H:(half + 1) * H], sel[:, u % UNITS, :],
                                                        bc[:, u // UNITS, 0 if kind == "b" else 1, half * H:(half + 1) * H],
                                                        start=True, stop=True)
                            last.then_inc(b_spread if kind == "b" else c_spread_pool if on_pool(u) else c_spread_vec, 1)

                        def reduce(u):
                            n = u % STATES
                            if n == 0:
                                t.wait_ge(y_ready, tiles + u // STATES + ONE)
                            wait_product(t, u, q_pool, q_vec)
                            for half in range(2):
                                last = nc.tensor.matmul(p_y[:, half * H:(half + 1) * H], eye[:],
                                                        hc[:, u % HC_SLOTS, half * H:(half + 1) * H],
                                                        start=(n == 0), stop=(n == STATES - 1))
                            last.then_inc(reduced, 1)

                        for step in range(ROUND + REDUCE_LAG):
                            if step < ROUND:
                                make("b", step)
                            if 1 <= step <= ROUND and on_pool(step - 1):
                                make("c", step - 1)
                            if 2 <= step < ROUND + 2 and not on_pool(step - 2):
                                make("c", step - 2)
                            if step >= REDUCE_LAG:
                                reduce(step - REDUCE_LAG)

            @block.vector
            def _(d):
                with d.Fori(0, DIRS) as k:
                    with d.Fori(0, ROUNDS) as r:
                        q = k * (SCAN_CHUNKS * UNITS) + r * ROUND
                        q_vec = k * (ROUNDS * R_VEC) + r * R_VEC
                        kept = k * ((SCAN_CHUNKS + 1) * UNITS) + r * ROUND + UNITS

                        def times_b(u):
                            s, v = divmod(u, UNITS)
                            if v == 0:
                                d.wait_ge(loaded[s], k * (LOADS * ROUNDS) + r * LOADS + LOADS + ONE)
                            d.wait_ge(b_spread, q + (u + 1) + ONE)
                            d.wait_ge(scanned, q + max(u - DBU_SLOTS + 1, 0) + ONE)
                            nc.vector.tensor_tensor(dbu[:, u % DBU_SLOTS, :], bank("b", u), du[:, s, v // STATES, :],
                                                    ALU.mult).then_inc(dbu_ready, 1)

                        def recur(u):
                            d.wait_ge(da_ready, q + (u + 1) + ONE)
                            d.wait_ge(dbu_ready, q + (u + 1) + ONE)
                            d.wait_ge(state_ready, kept + max(u - H_SLOTS + 1, 0) + ONE)
                            d.wait_ge(reduced, q + max(u - H_SLOTS + 1, 0) + ONE)
                            nc.vector.tensor_tensor_scan(h[:, u % H_SLOTS, :], da[:, u % DA_SLOTS, :], dbu[:, u % DBU_SLOTS, :],
                                                         state[:, u % UNITS:u % UNITS + 1], ALU.mult, ALU.add).then_inc(scanned, 1)

                        def times_c(u):
                            d.wait_ge(c_spread_vec, q_vec + (u - pool_units(u) + 1) + ONE)
                            d.wait_ge(scanned, q + (u + 1) + ONE)
                            d.wait_ge(reduced, q + max(u - HC_SLOTS + 1, 0) + ONE)
                            nc.vector.tensor_tensor(hc[:, u % HC_SLOTS, :], bank("c", u), h[:, u % H_SLOTS, :],
                                                    ALU.mult).then_inc(hc_vector, 1)

                        for step in range(ROUND + 2):
                            if step < ROUND:
                                times_b(step)
                            if 1 <= step <= ROUND:
                                recur(step - 1)
                            if step >= 2 and not on_pool(step - 2):
                                times_c(step - 2)


def merge(nc, l, w, u_d, useq_d, gate_d, y_d, ym_d, stat_d):
    with Phase(nc, f"merge{l}") as ph:
        gated = l == 1
        DW = CHUNK
        acc = ph.sb("acc", [P, 2, L])
        dskip = ph.sb("dskip", [P, TILES, DIRS])
        dsum = ph.sb("dsum", [P, TILES])
        y = ph.sb("y", [P, 2, DW])
        if gated:
            us = ph.sb("us", [P, 2, DW])
            gate = ph.sb("gate", [IMAGES * DIRS, L])
            gsel = ph.sb("gsel", [IMAGES * DIRS, DIRS, TILES, P])
            p_gate = [ph.ps(f"p_gate{j}", [P, 3, 512]) for j in range(2)]
        BN = 512
        NBN = L // BN
        if stat_d is not None:
            bn = ph.sb("bn", [P, NBN, 6])
            mv = ph.sb("mv", [P, TILES, 2])
        consts = ph.sem("consts")
        u_loaded = [ph.sem(f"u_loaded{m}") for m in range(TILES)]
        y_loaded = [ph.sem(f"y_loaded{j}") for j in range(2)]
        skip = ph.sem("skip")
        gated_y = ph.sem("gated_y")
        spread = ph.sem("spread")
        added = ph.sem("added")
        stats = ph.sem("stats")
        stored = [ph.sem(f"stored{m}") for m in range(TILES)]
        stat_stored = ph.sem("stat_stored")
        walks = WALKS[l]
        PAIRS = 2 if walks[0][0] == "window" or walks[0][2] == "snake" else 1
        PER = DIRS * CHUNKS
        Y_LOADS = 16 * (2 if gated else 1)
        with ph.block() as block:
            @block.sync
            def _(sp):
                sp.dma_start(dskip[:], w["dskip"]).then_inc(consts, 16)
                if gated:
                    sp.dma_start(gate[:], gate_d).then_inc(consts, 16)
                    sp.dma_start(gsel[:], w["gsel"]).then_inc(consts, 16)
                for m in range(TILES):
                    if not gated:
                        if m >= 2:
                            sp.wait_ge(stored[m - 2], 16 + ONE)
                        sp.dma_start(acc[:, m % 2, :], u_d[:, m, :]).then_inc(u_loaded[m], 16)
                    with sp.Fori(0, PER // 2) as i:
                        for j in range(2):
                            sp.wait_ge(added, i * (2 * PAIRS) + (m * PER + j + 1) * PAIRS + ONE)
                            at = i * (2 * DW) + j * DW
                            sp.dma_start(y[:, j, :], y_d[:, m, bass.ds(at, DW)]).then_inc(y_loaded[j], 16)
                            if gated:
                                sp.dma_start(us[:, j, :], useq_d[:, m, bass.ds(at, DW)]).then_inc(y_loaded[j], 16)
                    sp.wait_ge(added, (2 + (m + 1) * PER) * PAIRS + ONE)
                    if stat_d is not None:
                        sp.wait_ge(stats, (m + 1) * (NBN + 1) + ONE)
                    sp.dma_start(ym_d[:, m, :], acc[:, m % 2, :]).then_inc(stored[m], 16)
                if stat_d is not None:
                    sp.dma_start(stat_d, mv[:]).then_inc(stat_stored, 16)
                    sp.wait_ge(stat_stored, 16 + ONE)
                for m in range(TILES):
                    sp.wait_ge(stored[m], 16 + ONE)

            if gated:
                @block.tensor
                def _(t):
                    t.wait_ge(consts, 48 + ONE)
                    for m in range(TILES):
                        for k in range(DIRS):
                            with t.Fori(0, CHUNKS // 2) as i:
                                for j in range(2):
                                    it = i * 2 + ((m * DIRS + k) * CHUNKS + j)
                                    t.wait_ge(added, it + 1 + ONE)
                                    axis, down, minor = walks[k]
                                    for n in range(3):
                                        rows = SUB // SIDE
                                        c = i * 2 + j
                                        if down:
                                            first = c * (-MAJORS) + (SIDE - MAJORS + n * rows)
                                        else:
                                            first = c * MAJORS + n * rows
                                        g3 = gate[:].rearrange("p (r c) -> p r c", c=SIDE)
                                        if axis == "row":
                                            blk = g3[:, bass.ds(first, rows), :]
                                        else:
                                            blk = g3[:, :, bass.ds(first, rows)].rearrange("p r c -> p c r")
                                        last = nc.tensor.matmul(p_gate[j][:, n, 0:SUB], gsel[:, k, m, :], blk, start=True, stop=True)
                                    last.then_inc(spread, 1)

            @block.vector
            def _(d):
                d.sem_inc(added, 2 * PAIRS)
                d.wait_ge(consts, (48 if gated else 16) + ONE)
                nc.vector.tensor_reduce(dsum[:], dskip[:], mybir.AxisListType.X, ALU.add).then_inc(skip, 1)
                d.wait_ge(skip, 1 + ONE)
                for m in range(TILES):
                    grid = acc[:, m % 2, :].rearrange("p (r c) -> p r c", c=SIDE)
                    if gated:
                        if m >= 2:
                            d.wait_ge(stored[m - 2], 16 + ONE)
                        nc.vector.memset(acc[:, m % 2, :], 0.0).then_inc(skip, 1)
                    else:
                        d.wait_ge(u_loaded[m], 16 + ONE)
                        nc.vector.tensor_scalar(acc[:, m % 2, :], acc[:, m % 2, :], dsum[:, m:m + 1], None, ALU.mult).then_inc(skip, 1)
                    d.wait_ge(skip, m + 2 + ONE)
                    for k in range(DIRS):
                        with d.Fori(0, CHUNKS // 2) as i:
                            for j in range(2):
                                it = i * 2 + ((m * DIRS + k) * CHUNKS + j)
                                d.wait_ge(y_loaded[j], i * Y_LOADS + ((m * DIRS + k) * (CHUNKS // 2) + 1) * Y_LOADS + ONE)
                                if gated:
                                    nc.vector.scalar_tensor_tensor(out=y[:, j, :], in0=us[:, j, :], scalar=dskip[:, m, k:k + 1],
                                                                   in1=y[:, j, :], op0=ALU.mult, op1=ALU.add).then_inc(gated_y, 1)
                                    d.wait_ge(gated_y, it * 2 + 1 + ONE)
                                    d.wait_ge(spread, it + 1 + ONE)
                                    y3 = y[:, j, :].rearrange("p (n s) -> p n s", n=3)
                                    g3 = p_gate[j][:, :, 0:SUB]
                                    if walks[k][1]:
                                        g3 = g3[:, ::-1, ::-1]
                                    nc.vector.tensor_tensor(y3, y3, g3, ALU.mult).then_inc(gated_y, 1)
                                    d.wait_ge(gated_y, it * 2 + 2 + ONE)
                                d.wait_ge(added, it * PAIRS + 2 * PAIRS + ONE)
                                for dst, src in walk_pairs(walks[k], i * 2 + j, grid, y[:, j, :]):
                                    nc.vector.tensor_tensor(dst, dst, src, ALU.add).then_inc(added, 1)
                    if stat_d is not None:
                        d.wait_ge(added, (2 + (m + 1) * PER) * PAIRS + ONE)
                        if m:
                            d.wait_ge(stats, m * (NBN + 1) + ONE)
                        for n in range(NBN):
                            nc.vector.bn_stats(bn[:, n, :], acc[:, m % 2, n * BN:(n + 1) * BN]).then_inc(stats, 1)
                        d.wait_ge(stats, m * (NBN + 1) + NBN + ONE)
                        nc.vector.bn_aggr(mv[:, m, :], bn[:].rearrange("p n s -> p (n s)")).then_inc(stats, 1)


FEED_AVG = [[(0, 0), (2, 1)], [(1, 0), (2, 2)], [(0, 3), (1, 4), (2, 5)]]


def finish(nc, l, w, x_d, ym_d, z_d, stat_d, out_d):
    with Phase(nc, f"fin{l}") as ph:
        N = SUB
        STEPS = L // N
        layer_norm = l in (0, 3)
        ym = ph.sb("ym", [P, 2, TILES, N])
        z = ph.sb("z", [P, 2, TILES, N])
        x = ph.sb("x", [CH, 2, IMAGES, N])
        gb = ph.sb("gb", [P, 2, TILES])
        wo = ph.sb("wo", [P, 3, CH])
        avg = ph.sb("avg", [P, 6, P])
        yc = ph.sb("yc", [P, TILES, N])
        sq = ph.sb("sq", [P, TILES, N])
        t_ = ph.sb("t", [P, TILES, N])
        o = ph.sb("o", [CH, 2, IMAGES, N])
        eps = ph.sb("eps", [P, 1])
        if stat_d is not None:
            mv = ph.sb("mv", [P, TILES, 2])
            gmv = ph.sb("gmv", [P, TILES, 2])
            scl = ph.sb("scl", [P, TILES])
            sft = ph.sb("sft", [P, TILES])
            s1 = ph.sb("s1", [P, TILES])
        p_a = ph.ps("p_a", [P, TILES, 512])
        p_b = ph.ps("p_b", [P, TILES, 512])
        p_o = ph.ps("p_o", [CH, IMAGES, 512])
        consts = ph.sem("consts")
        loaded = [ph.sem(f"loaded{j}") for j in range(2)]
        head = ph.sem("head")
        mean_done = ph.sem("mean_done")
        centred = ph.sem("centred")
        squared = ph.sem("squared")
        var_done = ph.sem("var_done")
        dev_done = ph.sem("dev_done")
        inv_done = ph.sem("inv_done")
        normed = ph.sem("normed")
        affine = ph.sem("affine")
        gated = ph.sem("gated")
        projected = ph.sem("projected")
        out_ready = ph.sem("out_ready")
        stored = [ph.sem(f"stored{j}") for j in range(2)]
        N_CONST = 4 if stat_d is not None else 3
        LOADS = 48
        with ph.block() as block:
            @block.sync
            def _(sp):
                for dst, src in ((gb, w["ln_gb"]), (wo, w["wo"]), (avg, w["avg6"])):
                    sp.dma_start(dst[:], src).then_inc(consts, 16)
                if stat_d is not None:
                    sp.dma_start(mv[:], stat_d).then_inc(consts, 16)

                def load(at, j):
                    sp.dma_start(ym[:, j], ym_d[:, :, bass.ds(at, N)]).then_inc(loaded[j], 16)
                    sp.dma_start(z[:, j], z_d[:, :, bass.ds(at, N)]).then_inc(loaded[j], 16)
                    sp.dma_start(x[:, j], x_d[:, :, bass.ds(at, N)].rearrange("b c n -> c b n")).then_inc(loaded[j], 16)

                def store(at, j, it):
                    sp.wait_ge(out_ready, it + 1 + ONE)
                    sp.dma_start(out_d[:, :, bass.ds(at, N)].rearrange("b c n -> c b n"), o[:, j]).then_inc(stored[j], 16)

                for j in range(2):
                    load(j * N, j)
                with sp.Fori(0, STEPS // 2 - 1) as i:
                    for j in range(2):
                        store(i * (2 * N) + j * N, j, i * 2 + j)
                        load(i * (2 * N) + (j + 2) * N, j)
                for j in range(2):
                    store((STEPS - 2 + j) * N, j, STEPS - 2 + j)
                for j in range(2):
                    sp.wait_ge(stored[j], 16 * (STEPS // 2) + ONE)

            @block.tensor
            def _(t):
                t.wait_ge(consts, 16 * N_CONST + ONE)
                if stat_d is not None:
                    t.wait_ge(head, 3 + ONE)
                    for m in range(TILES):
                        for n, (src, blk) in enumerate(FEED_AVG[m]):
                            last = nc.tensor.matmul(p_a[:, m, 0:2], avg[:, blk, :], mv[:, src, :], start=(n == 0),
                                                    stop=(n == len(FEED_AVG[m]) - 1))
                    last.then_inc(head, 1)
                with t.Fori(0, STEPS // 2) as i:
                    for j in range(2):
                        it = i * 2 + j
                        if layer_norm:
                            t.wait_ge(loaded[j], i * LOADS + LOADS + ONE)
                            t.wait_ge(centred, it + ONE)
                            for m in range(TILES):
                                for n, (src, blk) in enumerate(FEED_AVG[m]):
                                    last = nc.tensor.matmul(p_a[:, m, 0:N], avg[:, blk, :], ym[:, j, src, :], start=(n == 0),
                                                            stop=(n == len(FEED_AVG[m]) - 1))
                            last.then_inc(mean_done, 1)
                            t.wait_ge(squared, it + 1 + ONE)
                            t.wait_ge(dev_done, it + ONE)
                            for m in range(TILES):
                                for n, (src, blk) in enumerate(FEED_AVG[m]):
                                    last = nc.tensor.matmul(p_b[:, m, 0:N], avg[:, blk, :], sq[:, src, :], start=(n == 0),
                                                            stop=(n == len(FEED_AVG[m]) - 1))
                            last.then_inc(var_done, 1)
                        t.wait_ge(gated, it + 1 + ONE)
                        t.wait_ge(out_ready, it + ONE)
                        for b in range(IMAGES):
                            nc.tensor.matmul(p_o[:, b, 0:N], wo[:, 0, :], t_[:, b, :], start=True, stop=False)
                            last = nc.tensor.matmul(p_o[:, b, 0:N], wo[:, 1 + b, :], t_[:, 2, :], start=False, stop=True)
                        last.then_inc(projected, 1)

            @block.scalar
            def _(a):
                a.wait_ge(consts, 16 * N_CONST + ONE)
                a.wait_ge(head, 1 + ONE)
                if stat_d is not None:
                    a.wait_ge(head, 7 + ONE)
                    nc.scalar.activation(s1[:], scl[:], ACT.Sqrt, bias=eps[:]).then_inc(head, 1)
                    a.wait_ge(head, 12 + ONE)
                with a.Fori(0, STEPS // 2) as i:
                    for j in range(2):
                        it = i * 2 + j
                        if layer_norm:
                            a.wait_ge(centred, it + 1 + ONE)
                            a.wait_ge(var_done, it + ONE)
                            a.wait_ge(normed, it + ONE)
                            nc.scalar.activation(sq[:], yc[:], ACT.Square).then_inc(squared, 1)
                            a.wait_ge(var_done, it + 1 + ONE)
                            nc.scalar.activation(sq[:], p_b[:, :, 0:N], ACT.Sqrt, bias=eps[:]).then_inc(dev_done, 1)
                            a.wait_ge(normed, it + 1 + ONE)
                            for m in range(TILES):
                                last = nc.scalar.activation(yc[:, m, :], yc[:, m, :], ACT.Identity, bias=gb[:, 1, m:m + 1],
                                                            scale=gb[:, 0, m:m + 1])
                                last.then_inc(affine, 1)
                        elif stat_d is not None:
                            a.wait_ge(loaded[j], i * LOADS + LOADS + ONE)
                            a.wait_ge(gated, it + ONE)
                            for m in range(TILES):
                                nc.scalar.activation(yc[:, m, :], ym[:, j, m, :], ACT.Identity, bias=sft[:, m:m + 1],
                                                     scale=scl[:, m:m + 1]).then_inc(affine, 1)

            @block.vector
            def _(d):
                nc.vector.memset(eps[:], 1e-6 if l == 2 else 1e-5).then_inc(head, 1)
                if stat_d is not None:
                    d.wait_ge(consts, 16 * N_CONST + ONE)
                    nc.vector.tensor_tensor(s1[:], mv[:, :, 0], mv[:, :, 0], ALU.mult).then_inc(head, 1)
                    d.wait_ge(head, 2 + ONE)
                    nc.vector.tensor_tensor(mv[:, :, 1], mv[:, :, 1], s1[:], ALU.add).then_inc(head, 1)
                    d.wait_ge(head, 4 + ONE)
                    nc.vector.tensor_copy(gmv[:], p_a[:, :, 0:2]).then_inc(head, 1)
                    d.wait_ge(head, 5 + ONE)
                    nc.vector.tensor_tensor(s1[:], gmv[:, :, 0], gmv[:, :, 0], ALU.mult).then_inc(head, 1)
                    d.wait_ge(head, 6 + ONE)
                    nc.vector.tensor_tensor(scl[:], gmv[:, :, 1], s1[:], ALU.subtract).then_inc(head, 1)
                    d.wait_ge(head, 8 + ONE)
                    nc.vector.reciprocal(scl[:], s1[:]).then_inc(head, 1)
                    d.wait_ge(head, 9 + ONE)
                    nc.vector.tensor_tensor(scl[:], scl[:], gb[:, 0, :], ALU.mult).then_inc(head, 1)
                    d.wait_ge(head, 10 + ONE)
                    nc.vector.tensor_tensor(s1[:], scl[:], gmv[:, :, 0], ALU.mult).then_inc(head, 1)
                    d.wait_ge(head, 11 + ONE)
                    nc.vector.tensor_tensor(sft[:], gb[:, 1, :], s1[:], ALU.subtract).then_inc(head, 1)
                with d.Fori(0, STEPS // 2) as i:
                    for j in range(2):
                        it = i * 2 + j
                        d.wait_ge(loaded[j], i * LOADS + LOADS + ONE)
                        src = yc
                        if layer_norm:
                            d.wait_ge(mean_done, it + 1 + ONE)
                            d.wait_ge(gated, it + ONE)
                            nc.vector.tensor_tensor(yc[:], ym[:, j], p_a[:, :, 0:N], ALU.subtract).then_inc(centred, 1)
                            d.wait_ge(dev_done, it + 1 + ONE)
                            nc.vector.reciprocal(sq[:], sq[:]).then_inc(inv_done, 1)
                            d.wait_ge(inv_done, it + 1 + ONE)
                            nc.vector.tensor_tensor(yc[:], yc[:], sq[:], ALU.mult).then_inc(normed, 1)
                            d.wait_ge(affine, i * 6 + (3 * j + 3) + ONE)
                            y_in = yc[:]
                        elif stat_d is not None:
                            d.wait_ge(affine, i * 6 + (3 * j + 3) + ONE)
                            y_in = yc[:]
                        else:
                            y_in = ym[:, j]
                        d.wait_ge(projected, it + ONE)
                        nc.vector.tensor_tensor(t_[:], y_in, z[:, j], ALU.mult).then_inc(gated, 1)
                        d.wait_ge(projected, it + 1 + ONE)
                        d.wait_ge(stored[j], i * 16 + ONE)
                        nc.vector.tensor_tensor(o[:, j], x[:, j], p_o[:, :, 0:N], ALU.add).then_inc(out_ready, 1)


def program(nc, w, x_in, x_out, layers):
    def dram(name, shape, dt=F32):
        return nc.dram_tensor(name, shape, dt, kind="Internal").ap()

    xs_d = dram("xs_d", [P, TILES, SIDE * PADDED])
    z_d = dram("z_d", [P, TILES, L])
    u_d = dram("u_d", [P, TILES, L])
    delta_d = dram("delta_d", [P, TILES, DIRS * L])
    du_d = dram("du_d", [P, TILES, DIRS * L])
    bc_d = dram("bc_d", [2, PARTS * IMAGES * STATES, DIRS * L], BF16)
    y_d = dram("y_d", [P, TILES, DIRS * L])
    ym_d = dram("ym_d", [P, TILES, L])
    useq_d = dram("useq_d", [P, TILES, DIRS * L])
    ln_d = dram("ln_d", [IMAGES, CH, L])
    gate_d = dram("gate_d", [IMAGES * DIRS, L])
    stat_d = dram("stat_d", [P, TILES, 2])
    mids = [dram(f"x_d{n}", [IMAGES, CH, L]) for n in range(len(layers) - 1)]
    xs = [x_in, *mids, x_out]
    for n, l in enumerate(layers):
        x, out = xs[n], xs[n + 1]
        wl = {k.split("_", 1)[1]: v for k, v in w.items() if k.startswith((f"l{l}_", "c_"))}
        if l == 1:
            norm_gate(nc, x, wl, ln_d, gate_d)
            project(nc, l, ln_d, wl, xs_d, z_d, True)
        else:
            project(nc, l, x, wl, xs_d, z_d, False)
        if l == 0:
            conv_sampled(nc, wl, xs_d, u_d)
        elif l != 1:
            conv_depthwise(nc, l, wl, xs_d, u_d)
        if l == 1:
            prepare(nc, l, wl, xs_d, PADDED, delta_d, du_d, bc_d, useq_d)
        else:
            prepare(nc, l, wl, u_d, SIDE, delta_d, du_d, bc_d, None)
        scan(nc, l, wl, delta_d, du_d, bc_d, y_d)
        merge(nc, l, wl, u_d, useq_d, gate_d, y_d, ym_d, stat_d if l == 2 else None)
        finish(nc, l, wl, x, ym_d, z_d, stat_d if l == 2 else None, out)


LO, HI = slice(0, P), slice(P, HID)
HH = HID - P


def per_tile(v):
    v = np.asarray(v)
    both = np.concatenate([v[HI], v[HI]], 0)
    return np.ascontiguousarray(np.stack([v[LO], v[LO], both], 1))


def blocks6(m):
    out = np.zeros((P, 6, P), np.float32)
    out[:, 0, :] = m[LO, LO]
    out[:HH, 1, :] = m[HI, LO]
    out[HH:, 2, :] = m[HI, LO]
    out[:, 3, :HH] = m[LO, HI]
    out[:, 4, HH:] = m[LO, HI]
    out[:HH, 5, :HH] = m[HI, HI]
    out[HH:, 5, HH:] = m[HI, HI]
    return out


def diagonals(taps):
    n = taps.shape[1]
    out = np.zeros((P, n, 2, P), np.float32)
    r = np.arange(P)
    t = per_tile(taps)
    for q in range(n):
        out[r, q, 0, r] = t[:, 0, q]
        out[r, q, 1, r] = t[:, 2, q]
    return out


def in_proj_layout(m):
    out = np.zeros((CH, 2, 3, P), np.float32)
    for half in range(2):
        part = m[:, half * HID:(half + 1) * HID]
        out[:, half, 0] = part[:, LO]
        out[:, half, 1, :HH] = part[:, HI]
        out[:, half, 2, HH:] = part[:, HI]
    return out


def x_proj_layout(m):
    out = np.zeros((P, DIRS, TILES, DBL_ROWS), np.float32)
    for k in range(DIRS):
        dt, b, c = m[k, :RANK].T, m[k, RANK:RANK + STATES].T, m[k, RANK + STATES:].T
        for img in range(IMAGES):
            rows = slice(0, P), slice(img * HH, (img + 1) * HH)
            for part, width, base in ((b, STATES, 0), (c, STATES, 2 * STATES), (dt, RANK, 4 * STATES)):
                cols = slice(base + img * width, base + (img + 1) * width)
                out[rows[0], k, img, cols] = part[LO]
                out[rows[1], k, 2, cols] = part[HI]
    return out


def dt_layout(m):
    out = np.zeros((IMAGES * RANK, DIRS, TILES, P), np.float32)
    for k in range(DIRS):
        for img in range(IMAGES):
            rows = slice(img * RANK, (img + 1) * RANK)
            out[rows, k, img, :] = m[k, LO].T
            out[rows, k, 2, img * HH:(img + 1) * HH] = m[k, HI].T
    return out


def out_proj_layout(m):
    out = np.zeros((P, 3, CH), np.float32)
    out[:, 0] = m[LO]
    out[:HH, 1] = m[HI]
    out[HH:, 2] = m[HI]
    return out


def constants():
    c = {}
    c["c_eye"] = np.eye(P, dtype=np.float32)
    c["c_avg"] = np.kron(np.eye(CH // GROUP), np.full((GROUP, GROUP), 1.0 / GROUP)).astype(np.float32)
    c["c_mean96"] = np.full((CH, CH), 1.0 / CH, np.float32)
    c["c_avg6"] = blocks6(np.full((HID, HID), 1.0 / HID, np.float32))
    sel = np.zeros((PARTS, IMAGES, STATES, TILES, STATES, P), np.float32)
    for n in range(STATES):
        sel[:, 0, n, 0, n, :] = 1
        sel[:, 1, n, 1, n, :] = 1
        sel[:, 0, n, 2, n, :HH] = 1
        sel[:, 1, n, 2, n, HH:] = 1
    c["c_sel"] = np.where(sel.reshape(PARTS * IMAGES * STATES, UNITS, P) > 0, 0x3F80, 0).astype(np.uint16)
    gsel = np.zeros((IMAGES, DIRS, DIRS, TILES, P), np.float32)
    for k in range(DIRS):
        gsel[0, k, k, 0, :] = 1
        gsel[1, k, k, 1, :] = 1
        gsel[0, k, k, 2, :HH] = 1
        gsel[1, k, k, 2, HH:] = 1
    c["c_gsel"] = gsel.reshape(IMAGES * DIRS, DIRS, TILES, P)
    osel = np.zeros((IMAGES, 2, 2, TILES, P), np.float32)
    for axis in range(2):
        osel[0, axis, axis, 0, :] = 1
        osel[1, axis, axis, 1, :] = 1
        osel[0, axis, axis, 2, :HH] = 1
        osel[1, axis, axis, 2, HH:] = 1
    c["c_off_sel"] = osel.reshape(IMAGES * 2, 2, TILES, P)
    return c


def a_layout(a):
    return np.ascontiguousarray(np.stack([per_tile(a[k]).reshape(P, UNITS) for k in range(DIRS)], 1))


def by_dir(v):
    return np.ascontiguousarray(np.stack([per_tile(v[k]) for k in range(DIRS)], 1))


def layouts(i, layers):
    w = dict(constants())

    def same(v):
        return np.stack([v] * DIRS, 0)

    def common(l, win, wx, wdt, dtb, alog, dskip, wo, gb):
        w[f"l{l}_win"] = in_proj_layout(win)
        w[f"l{l}_wx"] = x_proj_layout(wx)
        w[f"l{l}_wdt"] = dt_layout(wdt)
        w[f"l{l}_dtb"] = by_dir(dtb)
        w[f"l{l}_alog"] = a_layout(alog)
        w[f"l{l}_dskip"] = np.ascontiguousarray(by_dir(dskip).transpose(0, 2, 1))
        w[f"l{l}_wo"] = out_proj_layout(wo)
        w[f"l{l}_ln_gb"] = np.ascontiguousarray(np.stack([per_tile(gb[0]), per_tile(gb[1])], 1))

    if 0 in layers:
        g = {k[8:]: v for k, v in i.items() if k.startswith("L0_conv_")}
        common(0, g["in_proj_w"].T, g["x_proj_weight"], g["dt_projs_weight"], g["dt_projs_bias"],
               g["A_logs"].reshape(DIRS, HID, STATES), g["Ds"].reshape(DIRS, HID), g["out_proj_w"].T,
               (g["ln_gamma"], g["ln_beta"]))
        w["l0_taps"] = np.ascontiguousarray(np.stack(
            [blocks6(g["off1_w"][:, :, t // 3, t % 3].T) for t in range(TAPS)], 1))
        w["l0_bn"] = np.ascontiguousarray(np.stack(
            [per_tile(g[n]) for n in ("off1_b", "bn_gamma", "bn_beta", "bn_mean", "bn_var")], 1))
        off = g["off2_w"].reshape(2, HID).T
        ow = np.zeros((P, TILES, IMAGES * 2), np.float32)
        ow[:, 0, 0:2] = off[LO]
        ow[:, 1, 2:4] = off[LO]
        ow[:HH, 2, 0:2] = off[HI]
        ow[HH:, 2, 2:4] = off[HI]
        w["l0_off_w"] = ow
    if 1 in layers:
        g = {k[8:]: v for k, v in i.items() if k.startswith("L1_conv_")}
        common(1, g["in_proj_w"].T, same(g["x_proj_w"]), same(g["dt_proj_w"]), same(g["dt_proj_b"]),
               same(g["A_log"]), same(g["D"]), g["out_proj_w"].T, (g["D"], g["D"]))
        w["l1_taps"] = diagonals(g["conv_w"].reshape(HID, SEQ_TAPS))
        w["l1_conv_b"] = per_tile(g["conv_b"])
        w["l1_norm_gb"] = np.ascontiguousarray(np.stack([g["norm_g"], g["norm_b"]], 1))
        w["l1_gate_w1"] = np.ascontiguousarray(g["gate_w1"].T)
        w["l1_gate_w2"] = np.ascontiguousarray(g["gate_w2"].T)
        w["l1_gate_b1"] = np.ascontiguousarray(g["gate_b1"].reshape(GATE_HID, 1))
        w["l1_gate_b2"] = np.ascontiguousarray(np.broadcast_to(g["gate_b2"].reshape(1, DIRS), (P, DIRS)))
    if 2 in layers:
        g = {k[8:]: v for k, v in i.items() if k.startswith("L2_conv_")}
        common(2, g["in_proj_w"].T, g["x_proj_w"], g["dt_w"], g["dt_b"], g["A_logs"].reshape(DIRS, HID, STATES),
               g["Ds"].reshape(DIRS, HID), g["out_proj_w"].T, (g["gn_gamma"], g["gn_beta"]))
        w["l2_taps"] = diagonals(g["conv_w"].reshape(HID, TAPS))
        w["l2_conv_b"] = per_tile(g["conv_b"])
    if 3 in layers:
        g = {k[8:]: v for k, v in i.items() if k.startswith("L3_conv_")}
        common(3, g["in_proj_w"], g["x_proj_weight"].transpose(0, 2, 1), g["dt_proj_weight"], g["dt_proj_bias"],
               same(g["A_log"]), same(g["D_skip"]), g["out_proj_w"], (g["ln_gamma"], g["ln_beta"]))
        w["l3_taps"] = diagonals(g["conv_w"].reshape(HID, TAPS))
        w["l3_conv_b"] = per_tile(g["conv_b"])
    return {k: np.ascontiguousarray(v) for k, v in w.items()}


def build(nc, w, layers):
    f32 = mybir.dt.from_np(np.dtype(np.float32))
    x_in = nc.dram_tensor("in_x", [IMAGES, CH, L], f32, kind="ExternalInput").ap()
    args = {k: nc.dram_tensor(f"in_{k}", v.shape, mybir.dt.from_np(v.dtype), kind="ExternalInput").ap()
            for k, v in w.items()}
    x_out = nc.dram_tensor("out_x", [IMAGES, CH, L], f32, kind="ExternalOutput").ap()
    program(nc, args, x_in, x_out, layers)


def kernel(**inputs):
    import concourse.bacc as bacc
    from concourse.bass_utils import run_bass_kernel_spmd as run

    inputs = {k: np.asarray(v) for k, v in inputs.items()}
    layers = (0, 1, 2, 3)
    w = layouts(inputs, layers)
    nc = bacc.Bacc("TRN2", target_bir_lowering=False, num_devices=1)
    build(nc, w, layers)
    arrays = {f"in_{k}": v for k, v in w.items()}
    arrays["in_x"] = np.ascontiguousarray(inputs["x"].reshape(IMAGES, CH, L))
    r = run(nc, [arrays], core_ids=[0])
    return r.results[0]["out_x"].reshape(IMAGES, CH, SIDE, SIDE)
```
